# Optimizing a Trainium2 kernel written in Bass

```python
import numpy as np
import jax
import jax.numpy as jnp

def _softmax(x, axis=-1):
    return jax.nn.softmax(x, axis=axis)

def _gelu(x):
    return jax.nn.gelu(x, approximate=True)

def _silu(x):
    return jax.nn.silu(x)

def _sigmoid(x):
    return jax.nn.sigmoid(x)

def _layernorm(x, axis=-1, eps=1e-05):
    m = jnp.mean(x, axis=axis, keepdims=True)
    v = jnp.var(x, axis=axis, keepdims=True)
    return (x - m) / jnp.sqrt(v + eps)

def _scatter_add(tgt, idx, src, axis=0):
    return tgt.at[idx].add(src)

def _segment_sum(src, seg, n):
    return jax.ops.segment_sum(src, seg, n)
kernel_name = 'mk_xattn_seq_d4_seqx_r8_d54591'

def setup_inputs(seed: int=0):
    np.random.seed(seed)
    _w = jnp.asarray

    def _rec_inputs():
        import jax
        import jax.numpy as jnp
        _rk = jax.random.key(seed)
        x = -0.0005207 + 1.001 * jax.random.normal(jax.random.fold_in(_rk, 1), (4, 256, 256), jnp.float32)
        _lenS = 256 - jax.random.randint(jax.random.fold_in(_rk, 7), (4,), 0, max(1, 256 // 4) + 1, jnp.int32)
        _lenS2 = 512 - jax.random.randint(jax.random.fold_in(_rk, 8), (4,), 0, max(1, 512 // 4) + 1, jnp.int32)
        _ctx_2048P = jax.random.normal(jax.random.fold_in(_rk, 11), (4, 16, 256), jnp.float32)
        _ctx_2048c = jax.random.dirichlet(jax.random.fold_in(_rk, 511), 0.3 * jnp.ones((16,), jnp.float32), (4, 512))
        _ctx_2048t = jnp.einsum('bsk,bkd->bsd', _ctx_2048c, _ctx_2048P)
        _ctx_2048t = _ctx_2048t * jax.lax.rsqrt(jnp.mean(jnp.square(_ctx_2048t)) + 1e-12) * 0.953939
        ctx_2048 = 2.81802e-05 + 1.00001 * (_ctx_2048t + 0.3 * jax.random.normal(jax.random.fold_in(_rk, 611), (4, 512, 256), jnp.float32))
        _validS = jnp.arange(256)[None, :] < _lenS[:, None]
        _validS2 = jnp.arange(512)[None, :] < _lenS2[:, None]
        _causal = jnp.tril(jnp.ones((256, 256), dtype=bool))
        mask_Bx1xSxS2_ff0 = jnp.where(jnp.ones((4, 1, 256, 512), dtype=bool), 0.0, -1000000000.0).astype(jnp.float32)
        mask_BxS2_bf1 = jnp.ones((4, 512), dtype=bool)
        mask_BxS2_ik0 = jnp.where(jnp.broadcast_to(_validS2[:, :], (4, 512)), 0, 1).astype(jnp.int32)
        return (x, ctx_2048, mask_Bx1xSxS2_ff0, mask_BxS2_bf1, mask_BxS2_ik0)
    x, ctx_2048, mask_Bx1xSxS2_ff0, mask_BxS2_bf1, mask_BxS2_ik0 = _rec_inputs()

    def _L0_xattn_setup():
        import jax, jax.numpy as jnp
        import numpy as np
        B, Q, S1, S2 = (4, 32, 256, 256)
        D, H, K, F = (256, 16, 128, 1024)
        LN_EPS = 1e-05

        def _layer_norm(x, scale, offset):
            mu = jnp.mean(x, axis=-1, keepdims=True)
            var = jnp.var(x, axis=-1, keepdims=True)
            return (x - mu) * jax.lax.rsqrt(var + LN_EPS) * scale + offset

        def _cross_attention(q_in, kv_in, wq, bq, wk, bk, wv, bv, wo, bo, bias_k, bias_v):
            b, q_len, _ = q_in.shape
            t = kv_in.shape[1]
            qh = (q_in @ wq + bq).reshape(b, q_len, H, K)
            kh = (kv_in @ wk + bk).reshape(b, t, H, K)
            vh = (kv_in @ wv + bv).reshape(b, t, H, K)
            kh = jnp.concatenate([kh, jnp.broadcast_to(bias_k, (b, 1, H, K))], axis=1)
            vh = jnp.concatenate([vh, jnp.broadcast_to(bias_v, (b, 1, H, K))], axis=1)
            scale = jnp.sqrt(jnp.asarray(K, q_in.dtype))
            logits = jnp.einsum('bqhk,bthk->bhqt', qh, kh) / scale
            weights = jax.nn.softmax(logits, axis=-1)
            ctx = jnp.einsum('bhqt,bthk->bqhk', weights, vh).reshape(b, q_len, H * K)
            return ctx @ wo + bo

        def _forward(x, xf_1, xf_2, ln1_scale, ln1_offset, wq1, bq1, wk1, bk1, wv1, bv1, wo1, bo1, bias_k1, bias_v1, ln2_scale, ln2_offset, wq2, bq2, wk2, bk2, wv2, bv2, wo2, bo2, bias_k2, bias_v2, ln_mlp_scale, ln_mlp_offset, w_fc1, b_fc1, w_fc2, b_fc2):
            res = x
            h = _layer_norm(x, ln1_scale, ln1_offset)
            x = res + _cross_attention(h, xf_1, wq1, bq1, wk1, bk1, wv1, bv1, wo1, bo1, bias_k1, bias_v1)
            res = x
            h = _layer_norm(x, ln2_scale, ln2_offset)
            x = res + _cross_attention(h, xf_2, wq2, bq2, wk2, bk2, wv2, bv2, wo2, bo2, bias_k2, bias_v2)
            h = _layer_norm(x, ln_mlp_scale, ln_mlp_offset)
            h = jax.nn.gelu(h @ w_fc1 + b_fc1, approximate=False) @ w_fc2 + b_fc2
            return x + h
        key = jax.random.key(seed)
        ks = iter(jax.random.split(key, 64))

        def rn(shape, s=0.02):
            return jax.random.normal(next(ks), shape, jnp.float32) * s
        inp = {'x': rn((B, Q, D), 1.0), 'xf_1': rn((B, S1, D), 1.0), 'xf_2': rn((B, S2, D), 1.0)}
        for i in (1, 2):
            inp[f'ln{i}_scale'] = jnp.ones((D,), jnp.float32)
            inp[f'ln{i}_offset'] = jnp.zeros((D,), jnp.float32)
            inp[f'wq{i}'] = rn((D, H * K))
            inp[f'bq{i}'] = jnp.zeros((H * K,), jnp.float32)
            inp[f'wk{i}'] = rn((D, H * K))
            inp[f'bk{i}'] = jnp.zeros((H * K,), jnp.float32)
            inp[f'wv{i}'] = rn((D, H * K))
            inp[f'bv{i}'] = jnp.zeros((H * K,), jnp.float32)
            inp[f'wo{i}'] = rn((H * K, D))
            inp[f'bo{i}'] = jnp.zeros((D,), jnp.float32)
            inp[f'bias_k{i}'] = rn((1, 1, H, K))
            inp[f'bias_v{i}'] = rn((1, 1, H, K))
        inp['ln_mlp_scale'] = jnp.ones((D,), jnp.float32)
        inp['ln_mlp_offset'] = jnp.zeros((D,), jnp.float32)
        inp['w_fc1'] = rn((D, F))
        inp['b_fc1'] = jnp.zeros((F,), jnp.float32)
        inp['w_fc2'] = rn((F, D))
        inp['b_fc2'] = jnp.zeros((D,), jnp.float32)
        return inp
    _L0_xattn_all = _L0_xattn_setup()
    _L0_xattn_in = {k: v for k, v in _L0_xattn_all.items() if k in ('ln1_scale', 'ln1_offset', 'wq1', 'bq1', 'wk1', 'bk1', 'wv1', 'bv1', 'wo1', 'bo1', 'bias_k1', 'bias_v1', 'ln2_scale', 'ln2_offset', 'wq2', 'bq2', 'wk2', 'bk2', 'wv2', 'bv2', 'wo2', 'bo2', 'bias_k2', 'bias_v2', 'ln_mlp_scale', 'ln_mlp_offset', 'w_fc1', 'b_fc1', 'w_fc2', 'b_fc2')}
    del _L0_xattn_all

    def _L1_xattn_setup():
        import jax, jax.numpy as jnp
        import numpy as np
        H = 256
        NH = 32
        KVH = 8
        HD = H // NH
        GROUPS = NH // KVH
        EPS = 1e-06
        B, L, S = (4, 128, 128)

        def _gqa_forward(hidden_state, encoder_hidden_state, encoder_attention_mask, Wq, bq, Wk, bk, Wv, bv, Wo, bo, gamma, beta):
            b, l, _ = hidden_state.shape
            s = encoder_hidden_state.shape[1]
            q = hidden_state @ Wq + bq
            k = encoder_hidden_state @ Wk + bk
            v = encoder_hidden_state @ Wv + bv
            q = q.reshape(b, l, KVH, GROUPS, HD).transpose(0, 2, 3, 1, 4)
            k = k.reshape(b, s, KVH, HD).transpose(0, 2, 1, 3)
            v = v.reshape(b, s, KVH, HD).transpose(0, 2, 1, 3)
            scale = 1.0 / jnp.sqrt(jnp.asarray(HD, q.dtype))
            scores = jnp.einsum('bkgld,bksd->bkgls', q, k) * scale
            scores = scores + encoder_attention_mask[:, :, None, :, :]
            attn = jax.nn.softmax(scores, axis=-1)
            out = jnp.einsum('bkgls,bksd->bkgld', attn, v)
            out = out.transpose(0, 3, 1, 2, 4).reshape(b, l, H)
            out = out @ Wo + bo
            x = out + hidden_state
            mu = jnp.mean(x, axis=-1, keepdims=True)
            var = jnp.var(x, axis=-1, keepdims=True)
            return (x - mu) * jax.lax.rsqrt(var + EPS) * gamma + beta
        key = jax.random.key(seed)
        ks = jax.random.split(key, 12)
        sd = 0.02
        return {'hidden_state': jax.random.normal(ks[0], (B, L, H), jnp.float32), 'encoder_hidden_state': jax.random.normal(ks[1], (B, S, H), jnp.float32), 'encoder_attention_mask': jnp.zeros((B, 1, L, S), jnp.float32), 'Wq': jax.random.normal(ks[2], (H, H), jnp.float32) * sd, 'bq': jnp.zeros((H,), jnp.float32), 'Wk': jax.random.normal(ks[3], (H, KVH * HD), jnp.float32) * sd, 'bk': jnp.zeros((KVH * HD,), jnp.float32), 'Wv': jax.random.normal(ks[4], (H, KVH * HD), jnp.float32) * sd, 'bv': jnp.zeros((KVH * HD,), jnp.float32), 'Wo': jax.random.normal(ks[5], (H, H), jnp.float32) * sd, 'bo': jnp.zeros((H,), jnp.float32), 'gamma': jnp.ones((H,), jnp.float32), 'beta': jnp.zeros((H,), jnp.float32)}
    _L1_xattn_all = _L1_xattn_setup()
    _L1_xattn_in = {k: v for k, v in _L1_xattn_all.items() if k in ('Wq', 'bq', 'Wk', 'bk', 'Wv', 'bv', 'Wo', 'bo', 'gamma', 'beta')}
    del _L1_xattn_all

    def _L2_xattn_setup():
        import jax, jax.numpy as jnp
        import numpy as np
        HIDDEN = 256
        HEADS = 16
        HEAD_DIM = HIDDEN // HEADS
        LN_EPS = 1e-05
        GATE_INIT = 0.5

        def _layer_norm(x, gamma, beta):
            mu = jnp.mean(x, axis=-1, keepdims=True)
            var = jnp.mean(jnp.square(x - mu), axis=-1, keepdims=True)
            return (x - mu) * jax.lax.rsqrt(var + LN_EPS) * gamma + beta
        key = jax.random.key(seed)
        ks = jax.random.split(key, 8)
        B, T_TEXT, T_AUDIO = (4, 256, 1500)
        s = 0.02
        return {'hidden_states': jax.random.normal(ks[0], (B, T_TEXT, HIDDEN), jnp.float32), 'audio_kv': jax.random.normal(ks[1], (B, T_AUDIO, HIDDEN), jnp.float32), 'audio_attention_mask': jnp.ones((B, T_AUDIO), dtype=bool), 'Wq': jax.random.normal(ks[2], (HIDDEN, HIDDEN), jnp.float32) * s, 'Wk': jax.random.normal(ks[3], (HIDDEN, HIDDEN), jnp.float32) * s, 'Wv': jax.random.normal(ks[4], (HIDDEN, HIDDEN), jnp.float32) * s, 'Wo': jax.random.normal(ks[5], (HIDDEN, HIDDEN), jnp.float32) * s, 'ln_gamma': jnp.ones((HIDDEN,), jnp.float32), 'ln_beta': jnp.zeros((HIDDEN,), jnp.float32), 'gate': jnp.array([GATE_INIT], jnp.float32)}
    _L2_xattn_all = _L2_xattn_setup()
    _L2_xattn_in = {k: v for k, v in _L2_xattn_all.items() if k in ('Wq', 'Wk', 'Wv', 'Wo', 'ln_gamma', 'ln_beta', 'gate')}
    del _L2_xattn_all

    def _L3_xattn_setup():
        import jax, jax.numpy as jnp
        import numpy as np
        B, P, K, H, NH = (4, 256, 32, 256, 16)
        DH = H // NH
        EPS = 1e-06

        def rmsnorm(x, w):
            var = jnp.mean(jnp.square(x), axis=-1, keepdims=True)
            return x * jax.lax.rsqrt(var + EPS) * w
        key = jax.random.key(seed)
        ks = jax.random.split(key, 12)
        s = 0.02
        return {'x': jax.random.normal(ks[0], (B, P, H), jnp.float32), 'latents': jax.random.normal(ks[1], (B, K, H), jnp.float32), 'attention_mask': jax.random.randint(ks[2], (B, P), 0, 2, jnp.int32), 'q_w': s * jax.random.normal(ks[3], (H, H), jnp.float32), 'q_b': jnp.zeros((H,), jnp.float32), 'kv_w': s * jax.random.normal(ks[4], (H, 2 * H), jnp.float32), 'kv_b': jnp.zeros((2 * H,), jnp.float32), 'out_w': s * jax.random.normal(ks[5], (H, H), jnp.float32), 'out_b': jnp.zeros((H,), jnp.float32), 'postnorm_w': jnp.ones((H,), jnp.float32), 'mlp_w1': s * jax.random.normal(ks[6], (H, 4 * H), jnp.float32), 'mlp_b1': jnp.zeros((4 * H,), jnp.float32), 'mlp_w2': s * jax.random.normal(ks[7], (4 * H, H), jnp.float32), 'mlp_b2': jnp.zeros((H,), jnp.float32)}
    _L3_xattn_all = _L3_xattn_setup()
    _L3_xattn_in = {k: v for k, v in _L3_xattn_all.items() if k in ('q_w', 'q_b', 'kv_w', 'kv_b', 'out_w', 'out_b', 'postnorm_w', 'mlp_w1', 'mlp_b1', 'mlp_w2', 'mlp_b2')}
    del _L3_xattn_all
    return {'x': x, 'ctx_2048': ctx_2048, 'mask_Bx1xSxS2_ff0': mask_Bx1xSxS2_ff0, 'mask_BxS2_bf1': mask_BxS2_bf1, 'mask_BxS2_ik0': mask_BxS2_ik0, 'L0_xattn_ln1_scale': _L0_xattn_in['ln1_scale'], 'L0_xattn_ln1_offset': _L0_xattn_in['ln1_offset'], 'L0_xattn_wq1': _L0_xattn_in['wq1'], 'L0_xattn_bq1': _L0_xattn_in['bq1'], 'L0_xattn_wk1': _L0_xattn_in['wk1'], 'L0_xattn_bk1': _L0_xattn_in['bk1'], 'L0_xattn_wv1': _L0_xattn_in['wv1'], 'L0_xattn_bv1': _L0_xattn_in['bv1'], 'L0_xattn_wo1': _L0_xattn_in['wo1'], 'L0_xattn_bo1': _L0_xattn_in['bo1'], 'L0_xattn_bias_k1': _L0_xattn_in['bias_k1'], 'L0_xattn_bias_v1': _L0_xattn_in['bias_v1'], 'L0_xattn_ln2_scale': _L0_xattn_in['ln2_scale'], 'L0_xattn_ln2_offset': _L0_xattn_in['ln2_offset'], 'L0_xattn_wq2': _L0_xattn_in['wq2'], 'L0_xattn_bq2': _L0_xattn_in['bq2'], 'L0_xattn_wk2': _L0_xattn_in['wk2'], 'L0_xattn_bk2': _L0_xattn_in['bk2'], 'L0_xattn_wv2': _L0_xattn_in['wv2'], 'L0_xattn_bv2': _L0_xattn_in['bv2'], 'L0_xattn_wo2': _L0_xattn_in['wo2'], 'L0_xattn_bo2': _L0_xattn_in['bo2'], 'L0_xattn_bias_k2': _L0_xattn_in['bias_k2'], 'L0_xattn_bias_v2': _L0_xattn_in['bias_v2'], 'L0_xattn_ln_mlp_scale': _L0_xattn_in['ln_mlp_scale'], 'L0_xattn_ln_mlp_offset': _L0_xattn_in['ln_mlp_offset'], 'L0_xattn_w_fc1': _L0_xattn_in['w_fc1'], 'L0_xattn_b_fc1': _L0_xattn_in['b_fc1'], 'L0_xattn_w_fc2': _L0_xattn_in['w_fc2'], 'L0_xattn_b_fc2': _L0_xattn_in['b_fc2'], 'L1_xattn_Wq': _L1_xattn_in['Wq'], 'L1_xattn_bq': _L1_xattn_in['bq'], 'L1_xattn_Wk': _L1_xattn_in['Wk'], 'L1_xattn_bk': _L1_xattn_in['bk'], 'L1_xattn_Wv': _L1_xattn_in['Wv'], 'L1_xattn_bv': _L1_xattn_in['bv'], 'L1_xattn_Wo': _L1_xattn_in['Wo'], 'L1_xattn_bo': _L1_xattn_in['bo'], 'L1_xattn_gamma': _L1_xattn_in['gamma'], 'L1_xattn_beta': _L1_xattn_in['beta'], 'L2_xattn_Wq': _L2_xattn_in['Wq'], 'L2_xattn_Wk': _L2_xattn_in['Wk'], 'L2_xattn_Wv': _L2_xattn_in['Wv'], 'L2_xattn_Wo': _L2_xattn_in['Wo'], 'L2_xattn_ln_gamma': _L2_xattn_in['ln_gamma'], 'L2_xattn_ln_beta': _L2_xattn_in['ln_beta'], 'L2_xattn_gate': _L2_xattn_in['gate'], 'L3_xattn_q_w': _L3_xattn_in['q_w'], 'L3_xattn_q_b': _L3_xattn_in['q_b'], 'L3_xattn_kv_w': _L3_xattn_in['kv_w'], 'L3_xattn_kv_b': _L3_xattn_in['kv_b'], 'L3_xattn_out_w': _L3_xattn_in['out_w'], 'L3_xattn_out_b': _L3_xattn_in['out_b'], 'L3_xattn_postnorm_w': _L3_xattn_in['postnorm_w'], 'L3_xattn_mlp_w1': _L3_xattn_in['mlp_w1'], 'L3_xattn_mlp_b1': _L3_xattn_in['mlp_b1'], 'L3_xattn_mlp_w2': _L3_xattn_in['mlp_w2'], 'L3_xattn_mlp_b2': _L3_xattn_in['mlp_b2']}

def reference(x, ctx_2048, mask_Bx1xSxS2_ff0, mask_BxS2_bf1, mask_BxS2_ik0, L0_xattn_ln1_scale, L0_xattn_ln1_offset, L0_xattn_wq1, L0_xattn_bq1, L0_xattn_wk1, L0_xattn_bk1, L0_xattn_wv1, L0_xattn_bv1, L0_xattn_wo1, L0_xattn_bo1, L0_xattn_bias_k1, L0_xattn_bias_v1, L0_xattn_ln2_scale, L0_xattn_ln2_offset, L0_xattn_wq2, L0_xattn_bq2, L0_xattn_wk2, L0_xattn_bk2, L0_xattn_wv2, L0_xattn_bv2, L0_xattn_wo2, L0_xattn_bo2, L0_xattn_bias_k2, L0_xattn_bias_v2, L0_xattn_ln_mlp_scale, L0_xattn_ln_mlp_offset, L0_xattn_w_fc1, L0_xattn_b_fc1, L0_xattn_w_fc2, L0_xattn_b_fc2, L1_xattn_Wq, L1_xattn_bq, L1_xattn_Wk, L1_xattn_bk, L1_xattn_Wv, L1_xattn_bv, L1_xattn_Wo, L1_xattn_bo, L1_xattn_gamma, L1_xattn_beta, L2_xattn_Wq, L2_xattn_Wk, L2_xattn_Wv, L2_xattn_Wo, L2_xattn_ln_gamma, L2_xattn_ln_beta, L2_xattn_gate, L3_xattn_q_w, L3_xattn_q_b, L3_xattn_kv_w, L3_xattn_kv_b, L3_xattn_out_w, L3_xattn_out_b, L3_xattn_postnorm_w, L3_xattn_mlp_w1, L3_xattn_mlp_b1, L3_xattn_mlp_w2, L3_xattn_mlp_b2):
    import jax
    import jax.numpy as jnp

    def _L0_xattn_ref(x, xf_1, xf_2, ln1_scale, ln1_offset, wq1, bq1, wk1, bk1, wv1, bv1, wo1, bo1, bias_k1, bias_v1, ln2_scale, ln2_offset, wq2, bq2, wk2, bk2, wv2, bv2, wo2, bo2, bias_k2, bias_v2, ln_mlp_scale, ln_mlp_offset, w_fc1, b_fc1, w_fc2, b_fc2):
        import jax, jax.numpy as jnp
        import numpy as np
        B, Q, S1, S2 = (4, 32, 256, 256)
        D, H, K, F = (256, 16, 128, 1024)
        LN_EPS = 1e-05

        def _layer_norm(x, scale, offset):
            mu = jnp.mean(x, axis=-1, keepdims=True)
            var = jnp.var(x, axis=-1, keepdims=True)
            return (x - mu) * jax.lax.rsqrt(var + LN_EPS) * scale + offset

        def _cross_attention(q_in, kv_in, wq, bq, wk, bk, wv, bv, wo, bo, bias_k, bias_v):
            b, q_len, _ = q_in.shape
            t = kv_in.shape[1]
            qh = (q_in @ wq + bq).reshape(b, q_len, H, K)
            kh = (kv_in @ wk + bk).reshape(b, t, H, K)
            vh = (kv_in @ wv + bv).reshape(b, t, H, K)
            kh = jnp.concatenate([kh, jnp.broadcast_to(bias_k, (b, 1, H, K))], axis=1)
            vh = jnp.concatenate([vh, jnp.broadcast_to(bias_v, (b, 1, H, K))], axis=1)
            scale = jnp.sqrt(jnp.asarray(K, q_in.dtype))
            logits = jnp.einsum('bqhk,bthk->bhqt', qh, kh) / scale
            weights = jax.nn.softmax(logits, axis=-1)
            ctx = jnp.einsum('bhqt,bthk->bqhk', weights, vh).reshape(b, q_len, H * K)
            return ctx @ wo + bo

        def _forward(x, xf_1, xf_2, ln1_scale, ln1_offset, wq1, bq1, wk1, bk1, wv1, bv1, wo1, bo1, bias_k1, bias_v1, ln2_scale, ln2_offset, wq2, bq2, wk2, bk2, wv2, bv2, wo2, bo2, bias_k2, bias_v2, ln_mlp_scale, ln_mlp_offset, w_fc1, b_fc1, w_fc2, b_fc2):
            res = x
            h = _layer_norm(x, ln1_scale, ln1_offset)
            x = res + _cross_attention(h, xf_1, wq1, bq1, wk1, bk1, wv1, bv1, wo1, bo1, bias_k1, bias_v1)
            res = x
            h = _layer_norm(x, ln2_scale, ln2_offset)
            x = res + _cross_attention(h, xf_2, wq2, bq2, wk2, bk2, wv2, bv2, wo2, bo2, bias_k2, bias_v2)
            h = _layer_norm(x, ln_mlp_scale, ln_mlp_offset)
            h = jax.nn.gelu(h @ w_fc1 + b_fc1, approximate=False) @ w_fc2 + b_fc2
            return x + h
        return _forward(x, xf_1, xf_2, ln1_scale, ln1_offset, wq1, bq1, wk1, bk1, wv1, bv1, wo1, bo1, bias_k1, bias_v1, ln2_scale, ln2_offset, wq2, bq2, wk2, bk2, wv2, bv2, wo2, bo2, bias_k2, bias_v2, ln_mlp_scale, ln_mlp_offset, w_fc1, b_fc1, w_fc2, b_fc2)

    def _L1_xattn_ref(hidden_state, encoder_hidden_state, encoder_attention_mask, Wq, bq, Wk, bk, Wv, bv, Wo, bo, gamma, beta):
        import jax, jax.numpy as jnp
        import numpy as np
        H = 256
        NH = 32
        KVH = 8
        HD = H // NH
        GROUPS = NH // KVH
        EPS = 1e-06
        B, L, S = (4, 128, 128)

        def _gqa_forward(hidden_state, encoder_hidden_state, encoder_attention_mask, Wq, bq, Wk, bk, Wv, bv, Wo, bo, gamma, beta):
            b, l, _ = hidden_state.shape
            s = encoder_hidden_state.shape[1]
            q = hidden_state @ Wq + bq
            k = encoder_hidden_state @ Wk + bk
            v = encoder_hidden_state @ Wv + bv
            q = q.reshape(b, l, KVH, GROUPS, HD).transpose(0, 2, 3, 1, 4)
            k = k.reshape(b, s, KVH, HD).transpose(0, 2, 1, 3)
            v = v.reshape(b, s, KVH, HD).transpose(0, 2, 1, 3)
            scale = 1.0 / jnp.sqrt(jnp.asarray(HD, q.dtype))
            scores = jnp.einsum('bkgld,bksd->bkgls', q, k) * scale
            scores = scores + encoder_attention_mask[:, :, None, :, :]
            attn = jax.nn.softmax(scores, axis=-1)
            out = jnp.einsum('bkgls,bksd->bkgld', attn, v)
            out = out.transpose(0, 3, 1, 2, 4).reshape(b, l, H)
            out = out @ Wo + bo
            x = out + hidden_state
            mu = jnp.mean(x, axis=-1, keepdims=True)
            var = jnp.var(x, axis=-1, keepdims=True)
            return (x - mu) * jax.lax.rsqrt(var + EPS) * gamma + beta
        return _gqa_forward(hidden_state, encoder_hidden_state, encoder_attention_mask, Wq, bq, Wk, bk, Wv, bv, Wo, bo, gamma, beta)

    def _L2_xattn_ref(hidden_states, audio_kv, audio_attention_mask, Wq, Wk, Wv, Wo, ln_gamma, ln_beta, gate):
        import jax, jax.numpy as jnp
        import numpy as np
        HIDDEN = 256
        HEADS = 16
        HEAD_DIM = HIDDEN // HEADS
        LN_EPS = 1e-05
        GATE_INIT = 0.5

        def _layer_norm(x, gamma, beta):
            mu = jnp.mean(x, axis=-1, keepdims=True)
            var = jnp.mean(jnp.square(x - mu), axis=-1, keepdims=True)
            return (x - mu) * jax.lax.rsqrt(var + LN_EPS) * gamma + beta
        B, Tt, D = hidden_states.shape
        Ta = audio_kv.shape[1]
        scale = HEAD_DIM ** (-0.5)
        a = _layer_norm(audio_kv, ln_gamma, ln_beta)
        Q = (hidden_states @ Wq.T).reshape(B, Tt, HEADS, HEAD_DIM).transpose(0, 2, 1, 3)
        K = (a @ Wk.T).reshape(B, Ta, HEADS, HEAD_DIM).transpose(0, 2, 1, 3)
        V = (a @ Wv.T).reshape(B, Ta, HEADS, HEAD_DIM).transpose(0, 2, 1, 3)
        scores = jnp.einsum('bhtd,bhsd->bhts', Q, K) * scale
        mask = audio_attention_mask[:, None, None, :]
        scores = jnp.where(mask, scores, jnp.float32(-jnp.inf))
        attn = jax.nn.softmax(scores, axis=-1)
        out = jnp.einsum('bhts,bhsd->bhtd', attn, V)
        out = out.transpose(0, 2, 1, 3).reshape(B, Tt, D)
        out = out @ Wo.T
        return hidden_states + jnp.tanh(gate) * out

    def _L3_xattn_ref(x, latents, attention_mask, q_w, q_b, kv_w, kv_b, out_w, out_b, postnorm_w, mlp_w1, mlp_b1, mlp_w2, mlp_b2):
        import jax, jax.numpy as jnp
        import numpy as np
        B, P, K, H, NH = (4, 256, 32, 256, 16)
        DH = H // NH
        EPS = 1e-06

        def rmsnorm(x, w):
            var = jnp.mean(jnp.square(x), axis=-1, keepdims=True)
            return x * jax.lax.rsqrt(var + EPS) * w
        b, p, _ = x.shape
        k_len = latents.shape[1]
        residual = latents
        h = jnp.concatenate([x, latents], axis=1)
        q = (latents @ q_w + q_b).reshape(b, k_len, NH, DH)
        kv = (h @ kv_w + kv_b).reshape(b, p + k_len, NH, DH, 2)
        kmat, v = (kv[..., 0], kv[..., 1])
        attn = jnp.einsum('bkhd,bnhd->bhkn', q, kmat) / DH
        full_mask = jnp.concatenate([attention_mask.astype(bool), jnp.ones((b, k_len), bool)], axis=-1)
        attn = jnp.where(full_mask[:, None, None, :], attn, -jnp.inf)
        attn = jax.nn.softmax(attn.astype(jnp.float32), axis=-1).astype(q.dtype)
        attn_out = jnp.einsum('bhkn,bnhd->bkhd', attn, v).reshape(b, k_len, H)
        attn_out = attn_out @ out_w + out_b + residual
        out = rmsnorm(attn_out, postnorm_w)
        out = jax.nn.gelu(out @ mlp_w1 + mlp_b1) @ mlp_w2 + mlp_b2
        return out + residual
    x = _L0_xattn_ref(x, ctx_2048, ctx_2048, L0_xattn_ln1_scale, L0_xattn_ln1_offset, L0_xattn_wq1, L0_xattn_bq1, L0_xattn_wk1, L0_xattn_bk1, L0_xattn_wv1, L0_xattn_bv1, L0_xattn_wo1, L0_xattn_bo1, L0_xattn_bias_k1, L0_xattn_bias_v1, L0_xattn_ln2_scale, L0_xattn_ln2_offset, L0_xattn_wq2, L0_xattn_bq2, L0_xattn_wk2, L0_xattn_bk2, L0_xattn_wv2, L0_xattn_bv2, L0_xattn_wo2, L0_xattn_bo2, L0_xattn_bias_k2, L0_xattn_bias_v2, L0_xattn_ln_mlp_scale, L0_xattn_ln_mlp_offset, L0_xattn_w_fc1, L0_xattn_b_fc1, L0_xattn_w_fc2, L0_xattn_b_fc2)
    x = _L1_xattn_ref(x, ctx_2048, mask_Bx1xSxS2_ff0, L1_xattn_Wq, L1_xattn_bq, L1_xattn_Wk, L1_xattn_bk, L1_xattn_Wv, L1_xattn_bv, L1_xattn_Wo, L1_xattn_bo, L1_xattn_gamma, L1_xattn_beta)
    x = _L2_xattn_ref(x, ctx_2048, mask_BxS2_bf1, L2_xattn_Wq, L2_xattn_Wk, L2_xattn_Wv, L2_xattn_Wo, L2_xattn_ln_gamma, L2_xattn_ln_beta, L2_xattn_gate)
    x = _L3_xattn_ref(ctx_2048, x, mask_BxS2_ik0, L3_xattn_q_w, L3_xattn_q_b, L3_xattn_kv_w, L3_xattn_kv_b, L3_xattn_out_w, L3_xattn_out_b, L3_xattn_postnorm_w, L3_xattn_mlp_w1, L3_xattn_mlp_b1, L3_xattn_mlp_w2, L3_xattn_mlp_b2)
    return x

_drawn_inputs = setup_inputs


def setup_inputs(seed=0):
    import zlib

    import numpy as np

    out = dict(_drawn_inputs(seed))
    spreads = {'L0_xattn_ln1_scale': (1.0, 0.6),
     'L0_xattn_ln1_offset': (0.0, 0.8),
     'L0_xattn_bq1': (0.0, 0.8),
     'L0_xattn_bk1': (0.0, 2.0),
     'L0_xattn_bv1': (0.0, 0.1),
     'L0_xattn_bo1': (0.0, 0.1),
     'L0_xattn_ln2_scale': (1.0, 0.6),
     'L0_xattn_ln2_offset': (0.0, 0.8),
     'L0_xattn_bq2': (0.0, 0.8),
     'L0_xattn_bk2': (0.0, 2.0),
     'L0_xattn_bv2': (0.0, 0.1),
     'L0_xattn_bo2': (0.0, 0.1),
     'L0_xattn_ln_mlp_scale': (1.0, 0.6),
     'L0_xattn_ln_mlp_offset': (0.0, 0.692),
     'L0_xattn_b_fc1': (0.0, 0.1),
     'L0_xattn_b_fc2': (0.0, 0.1),
     'L1_xattn_bq': (0.0, 0.8),
     'L1_xattn_bk': (0.0, 2.0),
     'L1_xattn_bv': (0.0, 0.285),
     'L1_xattn_bo': (0.0, 0.1),
     'L1_xattn_gamma': (1.0, 0.2),
     'L1_xattn_beta': (0.0, 0.1),
     'L2_xattn_ln_gamma': (1.0, 0.6),
     'L2_xattn_ln_beta': (0.0, 0.8),
     'L3_xattn_q_b': (0.0, 2.0),
     'L3_xattn_kv_b': (0.0, 0.8),
     'L3_xattn_out_b': (0.0, 2.0),
     'L3_xattn_postnorm_w': (1.0, 0.6),
     'L3_xattn_mlp_b1': (0.0, 0.1),
     'L3_xattn_mlp_b2': (0.0, 0.1)}
    factors = {'L0_xattn_wq1': 8.0,
     'L0_xattn_wk1': 8.0,
     'L0_xattn_bias_k1': 64.0,
     'L0_xattn_bias_v1': 64.0,
     'L0_xattn_wq2': 8.0,
     'L0_xattn_wk2': 8.0,
     'L0_xattn_bias_k2': 64.0,
     'L0_xattn_bias_v2': 64.0,
     'L1_xattn_Wq': 8.0,
     'L1_xattn_Wk': 8.0,
     'L2_xattn_Wq': 8.0,
     'L2_xattn_Wk': 8.0,
     'L3_xattn_q_w': 8.0,
     'L3_xattn_kv_w': 8.0,
     'L3_xattn_out_w': 8.0}
    for name, (base, spread) in spreads.items():
        noise = np.random.default_rng([zlib.crc32(name.encode()), seed]).standard_normal(out[name].shape)
        drawn = base * np.exp(spread * noise) if base else spread * noise
        out[name] = jnp.asarray(drawn.astype(out[name].dtype))
    for name, factor in factors.items():
        out[name] = (out[name] * factor).astype(out[name].dtype)
    return out
```

```python
import numpy as np
import concourse.bass as bass
from concourse import mybir
from contextlib import ExitStack

FP32 = mybir.dt.float32
FP32R = mybir.dt.float32r
INT32 = mybir.dt.int32
UINT8 = mybir.dt.uint8
ALU = mybir.AluOpType
ACT = mybir.ActivationFunctionType
AX = mybir.AxisListType

P = 128
B, Q, S, D = 4, 256, 512, 256
T = B * Q
C = B * S
XT = T // P
KD = D // P
QT = Q // P
ST = S // P
EPS0 = 1e-5

H0, HD0 = 16, 128
NP0 = H0 // 2
SC0 = float(HD0) ** -0.5
PACK_COLS = 8
PACK_SEL = 2 * (H0 + 1)
N0 = 2 * B * QT
PACK_W = 8 * D + PACK_COLS + PACK_SEL
COL_BQ, COL_BK, COL_LV, COL_BV = (8 * D + 2 * i for i in range(4))
COL_SEL = 8 * D + PACK_COLS


def mm3(pe, out, lh, ll, rh, rl, start, stop):
    pe.matmul(out, lh, rh, start=start, stop=False)
    pe.matmul(out, lh, rl, start=False, stop=False)
    return pe.matmul(out, ll, rh, start=False, stop=stop)


def inverse_root(dve, chain, at, out, var, root, tmp):
    dve.reciprocal(out, root).then_inc(chain, 1)
    dve.wait_ge(chain, at + 1)
    dve.tensor_tensor(tmp, var, out, ALU.mult).then_inc(chain, 1)
    dve.wait_ge(chain, at + 2)
    dve.tensor_tensor(tmp, tmp, out, ALU.mult).then_inc(chain, 1)
    dve.wait_ge(chain, at + 3)
    dve.tensor_scalar(tmp, tmp, -0.5, 1.5, ALU.mult, ALU.add).then_inc(chain, 1)
    dve.wait_ge(chain, at + 4)
    dve.tensor_tensor(out, out, tmp, ALU.mult).then_inc(chain, 1)
    dve.wait_ge(chain, at + 5)


NEWTON = 5


def semaphores(nc, ctx, prefix=""):
    taken = []

    def clear():
        nc.clear_and_free_semaphores(taken)
        nc.all_engine_barrier()

    def make(name):
        taken.append(nc.alloc_semaphore(prefix + name))
        return taken[-1]

    ctx.callback(clear)
    return make




class Shared:

    def __init__(self, nc, ctx):
        sb = lambda n, s, d=FP32: ctx.enter_context(nc.sbuf_tensor(n, s, d))
        self.ident = sb("ident", [P, P])
        self.xs = sb("xs", [P, XT, D])
        self.ctx_hi = sb("ctx_hi", [P, KD, C], FP32R)
        self.ctx_lo = sb("ctx_lo", [P, KD, C], FP32R)
        self.bank = [ctx.enter_context(nc.psum_tensor(f"bank{i}", [P, 2, 512], FP32)) for i in range(4)]

    def one(self, n):
        return self.bank[n // 2][:, n % 2, :]


def load_stage(nc, sh, x_dram, ctx_dram):
    CT = C // P
    with ExitStack() as ctx:
        sem = semaphores(nc, ctx)
        ctok = ctx.enter_context(nc.sbuf_tensor("ctok", [P, CT, D], FP32))
        ident_ready, x_loaded, turned, high_ready, low_ready = map(
            sem, ("ident_ready", "x_loaded", "ctx_turned", "ctx_high_ready", "ctx_low_ready"))
        ctx_loaded = [sem(f"ctx_loaded{b}") for b in range(B)]
        block = ctx.enter_context(nc.Block())

        @block.sync
        def _(sp):
            for b in range(B):
                sp.dma_start(ctok[:, b * ST:(b + 1) * ST, :],
                             ctx_dram[b * S:(b + 1) * S, :].rearrange("(t p) d -> p t d", p=P)).then_inc(ctx_loaded[b], 16)
            sp.dma_start(sh.xs[:], x_dram.rearrange("(t p) d -> p t d", p=P)).then_inc(x_loaded, 16)
            sp.wait_ge(x_loaded, 16)

        @block.gpsimd
        def _(pool):
            pool.memset(sh.ident[:], 0.0).then_inc(ident_ready, 1)
            pool.wait_ge(ident_ready, 1)
            pool.affine_select(out=sh.ident[:], in_=sh.ident[:], compare_op=ALU.not_equal, fill=1.0, base=0,
                               pattern=[[-1, P]], channel_multiplier=1).then_inc(ident_ready, 1)

        @block.tensor
        def _(pe):
            pe.wait_ge(ident_ready, 2)
            for n in range(B * KD):
                b, k = n // KD, n % KD
                pe.wait_ge(ctx_loaded[b], 16)
                if n >= 8:
                    pe.wait_ge(low_ready, n - 7)
                for t in range(ST):
                    last = pe.transpose(sh.one(n % 8)[:, t * P:(t + 1) * P],
                                        ctok[:, b * ST + t, k * P:(k + 1) * P], sh.ident[:])
                last.then_inc(turned, 1)

        @block.scalar
        def _(act):
            for n in range(B * KD):
                b, k = n // KD, n % KD
                act.wait_ge(turned, n + 1)
                act.activation(sh.ctx_hi[:, k, b * S:(b + 1) * S], sh.one(n % 8), ACT.Copy).then_inc(high_ready, 1)

        @block.vector
        def _(dve):
            for n in range(B * KD):
                b, k = n // KD, n % KD
                dve.wait_ge(high_ready, n + 1)
                dve.tensor_tensor(sh.ctx_lo[:, k, b * S:(b + 1) * S], sh.one(n % 8),
                                  sh.ctx_hi[:, k, b * S:(b + 1) * S].bitcast(FP32), ALU.subtract).then_inc(low_ready, 1)


class Steps:

    def __init__(self, per, ahead=0):
        self.per, self.ahead = per, ahead

    def after(self, i, n):
        return i * self.per + (self.ahead + n + 1)


def chunks_of(g):
    b = g // 4
    made = {3: [("q", b + 2), ("k0", b + 2)], 0: [("k1", b + 1)], 2: [("v0", b + 1), ("v1", b + 1)], 1: []}[g % 4]
    return [x for x in made if x[1] <= B]


CHUNKS0 = [(kind, b) for b in range(B) for kind in ("q", "k0", "k1", "v0", "v1")]
EARLY0 = CHUNKS0[:5]


def mixes_of(g):
    return ([("mix", (g - 3) // 2)] if g % 2 and g > 1 else []) + ([("u", 0)] if g == 4 else []) \
        + ([("out", g // 4 - 1)] if g % 4 == 2 and g > 2 else [])


LATE0 = [("mix", 2 * B - 1), ("out", B - 1)]
MIXES0 = [x for g in range(N0) for x in mixes_of(g)] + LATE0


def attention0(nc, sh, packs, ln_cols, u_init, wq_dram, lk_dram, bq_lk_dram, passes=2, pairs=NP0):
    NC, NM = len(CHUNKS0), len(MIXES0)
    n_chunk = {x: n for n, x in enumerate(CHUNKS0)}
    n_chunk |= {(kind, B): n + NC for (kind, b), n in list(n_chunk.items()) if b == 0}
    n_mix = {x: n for n, x in enumerate(MIXES0)}
    CH = Steps(NC)
    CH1 = Steps(NC, NC)
    MX = Steps(NM, NM)
    n_of_mixed = {("mix", u): u for u in range(2 * B)}
    MH = Steps(2 * B)
    TILE = Steps(N0)
    DEN = Steps(2 * N0)
    TILE1 = Steps(N0, N0)
    with ExitStack() as ctx:
        sb = lambda n, s, d=FP32: ctx.enter_context(nc.sbuf_tensor(n, s, d))
        sem = semaphores(nc, ctx)
        raw = sb("raw", [P, PACK_W])
        w_hi, w_lo = sb("w_hi", [P, 8, D], FP32R), sb("w_lo", [P, 8, D], FP32R)
        cols = sb("cols", [P, PACK_COLS])
        wq_all = sb("wq_all", [P, KD, H0 * HD0])
        lk_rows = sb("lk_rows", [P, H0 * HD0])
        bq_lk = sb("bq_lk", [H0, 2, HD0])
        wq_lk = sb("wq_lk", [P, KD, H0])
        lk_bias = sb("lk_bias", [H0, 1])
        lk_logit_t = sb("lk_logit_t", [H0, T])
        lk_logit = sb("lk_logit", [P, XT, H0])
        lk_pair = sb("lk_pair", [P, XT, 2])
        learned = sb("learned", [P, 2, H0 + 1])
        lncol = sb("lncol", [P, 2, KD])
        stats, mv, rstd = sb("stats", [P, XT, 6]), sb("mv", [P, XT, 2]), sb("rstd", [P, XT])
        var, root, newton = sb("var", [P, XT]), sb("root", [P, XT]), sb("newton", [P, XT])
        xn = sb("xn", [P, XT, D])
        h_full = sb("h_full", [P, KD, T])
        h_hi, h_lo = sb("h_hi", [P, KD, T], FP32R), sb("h_lo", [P, KD, T], FP32R)
        q_hi, q_lo = sb("q_hi", [P, 2, 2, Q], FP32R), sb("q_lo", [P, 2, 2, Q], FP32R)
        k_hi, k_lo = sb("k_hi", [P, 2, 2, S], FP32R), sb("k_lo", [P, 2, 2, S], FP32R)
        v_hi, v_lo = sb("v_hi", [P, 2, ST, D], FP32R), sb("v_lo", [P, 2, ST, D], FP32R)
        zeros = sb("zeros", [P, 1])
        junk = sb("junk", [P, 2, S])
        NPB = 4
        neg_max, total, learned_e, denom = (sb(n, [P, NPB]) for n in ("neg_max", "total", "learned_e", "denom"))
        probs = sb("probs", [P, NPB, S])
        pt_hi, pt_lo = sb("pt_hi", [P, 2, ST, Q], FP32R), sb("pt_lo", [P, 2, ST, Q], FP32R)
        o_hi, o_lo = sb("o_hi", [P, 2, Q], FP32R), sb("o_lo", [P, 2, Q], FP32R)
        learned_p = sb("learned_p", [P, XT, H0 + 1])
        learned_pt = sb("learned_pt", [H0 + 1, T])
        u_acc = sb("u_acc", [H0 + 1, D])

        names = ("raw_qkv_loaded raw_o_loaded const_loaded ln_loaded ones_ready qkv_high qkv_split pair_cols_ready "
                 "o_high o_split column_steps pair_logit_ready learned_ready stats_done mv_ready var_ready root_ready rstd_steps xn_ready "
                 "h_turned h_scaled h_high h_ready chunk_done chunk_high chunk_ready mix_done mix_high mix_ready scores_ready max_ready exp_ready "
                 "learned_e_ready denom_steps wq_all_loaded wq_lk_steps lk_done lk_scaled lk_turned lk_logit_ready probs_ready learned_copied turned pt_high pt_ready lp_turned lp_copied lp_out xs_final waits_taken_dve waits_taken_pe waits_taken_pool")
        (raw_qkv_loaded, raw_o_loaded, const_loaded, ln_loaded, ones_ready, qkv_high, qkv_split, pair_cols_ready,
         o_high, o_split, column_steps, pair_logit_ready, learned_ready, stats_done, mv_ready, var_ready, root_ready, rstd_steps, xn_ready,
         h_turned, h_scaled, h_high, h_ready, chunk_done, chunk_high, chunk_ready, mix_done, mix_high, mix_ready, scores_ready, max_ready, exp_ready,
         learned_e_ready, denom_steps, wq_all_loaded, wq_lk_steps, lk_done, lk_scaled, lk_turned, lk_logit_ready, probs_ready, learned_copied, turned, pt_high, pt_ready, lp_turned, lp_copied, lp_out,
         xs_final, waits_taken_dve, waits_taken_pe, waits_taken_pool) = map(sem, names.split())
        block = ctx.enter_context(nc.Block())
        s_bank = lambda g: sh.one(g % 3)
        t_bank = lambda g: sh.one(3 + g % 2)
        c_bank = lambda n: sh.one(5 + n % 2)
        m_bank = sh.one(7)
        tile_before = lambda g: g - 3 if g >= 3 else max(x for x in range(-3, 0) if (x + N0) % 3 == g)

        @block.sync
        def _(sp):
            def load_qkv(it):
                sp.dma_start(raw[:, 0:6 * D], packs[bass.ds(it, 1), :, 0:6 * D].rearrange("o p n -> (o p) n"))\
                  .then_inc(raw_qkv_loaded, 16)

            def load_o(it):
                sp.dma_start(raw[:, 6 * D:PACK_W], packs[bass.ds(it, 1), :, 6 * D:PACK_W].rearrange("o p n -> (o p) n"))\
                  .then_inc(raw_o_loaded, 16)

            def load_wq(a):
                sp.dma_start(wq_all[:], wq_dram[a].rearrange("(k p) n -> p k n", p=P)).then_inc(wq_all_loaded, 16)
                sp.dma_start(lk_rows[:], lk_dram[a:a + 1, :].partition_broadcast(P)).then_inc(wq_all_loaded, 16)
                sp.dma_start(bq_lk[:], bq_lk_dram[a]).then_inc(wq_all_loaded, 16)

            def load_norm(a):
                sp.dma_start(lncol[:], ln_cols[a]).then_inc(ln_loaded, 16)
                sp.dma_start(u_acc[:], u_init[a]).then_inc(const_loaded, 16)

            load_norm(0)
            load_qkv(0)
            load_wq(0)
            load_o(0)
            for a in range(passes):
                if a > 0:
                    sp.wait_ge(xs_final, a * 4 + 1)
                    load_norm(a)
                if a + 1 < passes:
                    sp.wait_ge(wq_lk_steps, a + 1)
                    load_wq(a + 1)
                with sp.Fori(0, pairs) as hp:
                    it = a * pairs + hp
                    sp.wait_ge(qkv_split, (it + 1) * 6)
                    load_qkv(it + 1)
                    sp.wait_ge(o_split, it + 1)
                    sp.wait_ge(mix_done, MX.after(it, n_mix["u", 0]))
                    load_o(it + 1)
            sp.wait_ge(raw_qkv_loaded, (passes * pairs + 1) * 16)
            sp.wait_ge(raw_o_loaded, (passes * pairs + 1) * 16)

        @block.gpsimd
        def _(pool):
            raw_w = raw[:, 0:8 * D].rearrange("p (n d) -> p n d", d=D)

            def split_qkv(nth, n):
                pool.nop().then_inc(waits_taken_pool, 1)
                pool.tensor_copy(w_hi[:, n, :], raw_w[:, n, :]).then_inc(qkv_high, 1)
                pool.wait_ge(qkv_high, nth * 6 + n + 1)
                last = pool.tensor_tensor(w_lo[:, n, :], raw_w[:, n, :], w_hi[:, n, :].bitcast(FP32), ALU.subtract)
                last.then_inc(qkv_split, 1)

            def small_columns(nth):
                pool.nop().then_inc(waits_taken_pool, 1)
                pool.tensor_copy(cols[:], raw[:, 8 * D:8 * D + PACK_COLS]).then_inc(pair_cols_ready, 1)
                for hh in range(2):
                    sel = raw[:, COL_SEL + hh * (H0 + 1):COL_SEL + (hh + 1) * (H0 + 1)]
                    pool.tensor_scalar(learned[:, hh, :], sel, raw[:, COL_LV + hh:COL_LV + hh + 1],
                                       raw[:, COL_BV + hh:COL_BV + hh + 1], ALU.mult, ALU.subtract)\
                        .then_inc(column_steps, 1)
                pool.wait_ge(column_steps, nth * 4 + 2)
                for hh in range(2):
                    sel = raw[:, COL_SEL + hh * (H0 + 1):COL_SEL + (hh + 1) * (H0 + 1)]
                    pool.tensor_tensor(learned[:, hh, :], learned[:, hh, :], sel, ALU.mult).then_inc(column_steps, 1)
                pool.wait_ge(column_steps, nth * 4 + 4)
                pool.nop().then_inc(waits_taken_pool, 1)
                for hh in range(2):
                    last = pool.tensor_copy(learned[:, hh, H0:H0 + 1], raw[:, COL_BV + hh:COL_BV + hh + 1])
                last.then_inc(learned_ready, 1)

            pool.nop().then_inc(learned_copied, N0)
            pool.memset(zeros[:], 0.0).then_inc(ones_ready, 1)
            pool.memset(learned_p[:], 1.0).then_inc(ones_ready, 1)
            pool.wait_ge(raw_qkv_loaded, 16)
            for n in range(6):
                split_qkv(0, n)
            pool.wait_ge(raw_o_loaded, 16)
            small_columns(0)
            with pool.Fori(0, passes) as a:
                with pool.Fori(0, pairs) as hp:
                    it = a * pairs + hp
                    pool.wait_ge(lk_logit_ready, a + 1)
                    pool.wait_ge(learned_e_ready, TILE1.after(it, -1))
                    pool.tensor_copy(lk_pair[:], lk_logit[:, :, bass.ds(hp * 2, 2)]).then_inc(pair_logit_ready, 1)
                    for g in range(N0):
                        b, hh, qt = g // 4, g // 2 % 2, g % 2
                        pool.wait_ge(denom_steps, DEN.after(it, 2 * g + 1))
                        pool.tensor_tensor(probs[:, g % NPB, :], probs[:, g % NPB, :],
                                           denom[:, g % NPB:g % NPB + 1].broadcast_to([P, S]), ALU.mult)\
                            .then_inc(probs_ready, 1)
                        pool.tensor_tensor(learned_p[:, b * QT + qt, bass.ds(hp * 2 + hh, 1)],
                                           learned_e[:, g % NPB:g % NPB + 1], denom[:, g % NPB:g % NPB + 1], ALU.mult)\
                            .then_inc(learned_copied, 1)
                        if g in (3, 4):
                            n = g - 3
                            if n == 0:
                                pool.wait_ge(raw_o_loaded, (it + 1) * 16)
                                pool.wait_ge(mix_done, MX.after(it, -1))
                                pool.nop().then_inc(waits_taken_pool, 1)
                            pool.tensor_copy(w_hi[:, 6 + n, :], raw_w[:, 6 + n, :]).then_inc(o_high, 1)
                            pool.wait_ge(o_high, it * 2 + n + 1)
                            last = pool.tensor_tensor(w_lo[:, 6 + n, :], raw_w[:, 6 + n, :],
                                                      w_hi[:, 6 + n, :].bitcast(FP32), ALU.subtract)
                            if n == 1:
                                last.then_inc(o_split, 1)
                        if g == 8:
                            pool.wait_ge(raw_qkv_loaded, (it + 2) * 16)
                            pool.wait_ge(chunk_done, CH.after(it, n_chunk["q", B - 1]))
                            split_qkv(it + 1, 0)
                            split_qkv(it + 1, 1)
                        if g == 9:
                            pool.wait_ge(chunk_done, CH.after(it, n_chunk["k1", B - 1]))
                            split_qkv(it + 1, 2)
                        if g == 10:
                            split_qkv(it + 1, 3)
                            pool.wait_ge(raw_o_loaded, (it + 2) * 16)
                            pool.wait_ge(chunk_ready, CH1.after(it, n_chunk["k1", B - 1]))
                            small_columns(it + 1)
                        if g in (12, 13):
                            if g == 12:
                                pool.wait_ge(chunk_done, CH.after(it, n_chunk["v1", B - 1]))
                            split_qkv(it + 1, g - 8)

        @block.tensor
        def _(pe):
            def chunk(it, x):
                kind, b = x
                n, b = n_chunk[x], b % B
                pe.wait_ge(chunk_ready, CH1.after(it, n - 2))
                pe.wait_ge(qkv_split, (it + n // NC) * 6 + {"q": 2, "k": 4, "v": 6}[kind[0]])
                out = c_bank(n)
                if kind == "q":
                    for hh in range(2):
                        for k in range(KD):
                            last = mm3(pe, out[:, hh * Q:(hh + 1) * Q],
                                       w_hi[:, k, hh * P:(hh + 1) * P], w_lo[:, k, hh * P:(hh + 1) * P],
                                       h_hi[:, k, b * Q:(b + 1) * Q], h_lo[:, k, b * Q:(b + 1) * Q], k == 0, k == KD - 1)
                elif kind in ("k0", "k1"):
                    hh = int(kind[1])
                    for k in range(KD):
                        last = mm3(pe, out, w_hi[:, 2 + k, hh * P:(hh + 1) * P], w_lo[:, 2 + k, hh * P:(hh + 1) * P],
                                   sh.ctx_hi[:, k, b * S:(b + 1) * S], sh.ctx_lo[:, k, b * S:(b + 1) * S], k == 0, k == KD - 1)
                else:
                    for j in range(2):
                        at = b * S + (2 * int(kind[1]) + j) * P
                        for k in range(KD):
                            last = mm3(pe, out[:, j * D:(j + 1) * D], sh.ctx_hi[:, k, at:at + P], sh.ctx_lo[:, k, at:at + P],
                                       w_hi[:, 4 + k, :], w_lo[:, 4 + k, :], k == 0, k == KD - 1)
                last.then_inc(chunk_done, 1)

            def mix(it, x):
                kind, b = x
                n = n_mix[x]
                pe.wait_ge(mix_ready, MX.after(it, n - 1))
                out = m_bank
                if kind == "u":
                    pe.wait_ge(learned_ready, it + 1)
                    pe.wait_ge(raw_o_loaded, (it + 1) * 16)
                    for hh in range(2):
                        last = pe.matmul(out[0:H0 + 1, 0:D], learned[:, hh, :],
                                         raw[:, (6 + hh) * D:(7 + hh) * D], start=hh == 0, stop=hh == 1)
                elif kind == "mix":
                    u, b = b, b // 2
                    hh = u % 2
                    pe.wait_ge(pt_ready, TILE1.after(it, 2 * u + 1))
                    pe.wait_ge(chunk_ready, CH1.after(it, n_chunk["v1", b]))
                    for s in range(ST):
                        last = mm3(pe, out[:, 0:Q], v_hi[:, b % 2, s, hh * P:(hh + 1) * P], v_lo[:, b % 2, s, hh * P:(hh + 1) * P],
                                   pt_hi[:, u % 2, s, :], pt_lo[:, u % 2, s, :], s == 0, s == ST - 1)
                else:
                    pe.wait_ge(o_split, it + 1)
                    pe.wait_ge(mix_ready, MX.after(it, n_mix["mix", 2 * b + 1]))
                    for qt in range(QT):
                        for hh in range(2):
                            last = mm3(pe, out[:, qt * D:(qt + 1) * D],
                                       o_hi[:, hh, qt * P:(qt + 1) * P], o_lo[:, hh, qt * P:(qt + 1) * P],
                                       w_hi[:, 6 + hh, :], w_lo[:, 6 + hh, :], hh == 0, hh == 1)
                last.then_inc(mix_done, 1)

            def scores(it, g):
                b, hh, qt = g // 4, g // 2 % 2, g % 2
                if g % 2 == 0:
                    pe.wait_ge(chunk_ready, CH1.after(it, n_chunk[f"k{hh}", b]))
                pe.wait_ge(exp_ready, TILE1.after(it, tile_before(g)))
                mm3(pe, s_bank(g), q_hi[:, b % 2, hh, qt * P:(qt + 1) * P], q_lo[:, b % 2, hh, qt * P:(qt + 1) * P],
                    k_hi[:, b % 2, hh, :], k_lo[:, b % 2, hh, :], True, True).then_inc(scores_ready, 1)

            def turn(it, g):
                pe.wait_ge(probs_ready, TILE.after(it, g))
                pe.wait_ge(pt_ready, TILE1.after(it, g - 2))
                for s in range(ST):
                    last = pe.transpose(t_bank(g)[:, s * P:(s + 1) * P], probs[:, g % NPB, s * P:(s + 1) * P], sh.ident[:])
                last.then_inc(turned, 1)

            def round_of(it, first=False, last=False):
                scores(it, 0)
                scores(it, 1)
                chunk(it, ("q", 1))
                chunk(it, ("k0", 1))
                if not first:
                    mix(it - 1, LATE0[0])
                scores(it, 2)
                if not first:
                    mix(it - 1, LATE0[1])
                for g in range(N0):
                    if g + 3 < N0:
                        scores(it, g + 3)
                    for x in chunks_of(g):
                        if not (last and x[1] == B):
                            chunk(it, x)
                    turn(it, g)
                    for x in mixes_of(g):
                        mix(it, x)

            pe.nop().then_inc(turned, N0)
            pe.nop().then_inc(mix_done, NM)
            with pe.Fori(0, passes) as a:
                pe.wait_ge(xn_ready, (a + 1) * XT)
                for k in range(KD):
                    for t in range(XT):
                        last = pe.transpose(sh.bank[k][:, t // 4, t % 4 * P:(t % 4 + 1) * P],
                                            xn[:, t, k * P:(k + 1) * P], sh.ident[:])
                    last.then_inc(h_turned, 1)
                pe.wait_ge(h_ready, (a + 1) * KD)
                for x in EARLY0:
                    chunk(a * pairs, x)
                pe.wait_ge(h_scaled, (a + 1) * KD)
                pe.wait_ge(wq_lk_steps, a + 1)
                for c in range(2):
                    for k in range(KD):
                        last = pe.matmul(sh.bank[0][0:H0, c, :], wq_lk[:, k, :], h_full[:, k, c * 512:(c + 1) * 512],
                                         start=k == 0, stop=k == KD - 1)
                last.then_inc(lk_done, 1)
                pe.wait_ge(lk_scaled, a + 1)
                pe.nop().then_inc(waits_taken_pe, 1)
                for t in range(XT):
                    last = pe.transpose(sh.bank[1][:, 0, t * H0:(t + 1) * H0], lk_logit_t[:, t * P:(t + 1) * P],
                                        sh.ident[0:H0, 0:H0])
                last.then_inc(lk_turned, 1)
                pe.wait_ge(lk_logit_ready, a + 1)
                round_of(a * pairs, first=True)
                with pe.Fori(1, pairs - 1) as hp:
                    round_of(a * pairs + hp)
                round_of(a * pairs + (pairs - 1), last=True)
                for x in LATE0:
                    mix(a * pairs + (pairs - 1), x)
                pe.wait_ge(learned_copied, (a + 1) * (pairs * N0) + N0)
                pe.wait_ge(mix_ready, (a + 1) * (pairs * NM) + NM)
                for t in range(XT):
                    last = pe.transpose(sh.bank[0][0:H0 + 1, t // 4, t % 4 * P:(t % 4 + 1) * P],
                                        learned_p[:, t, :], sh.ident[:])
                last.then_inc(lp_turned, 1)
                pe.wait_ge(lp_copied, a + 1)
                for t in range(XT):
                    last = pe.matmul(sh.one(4 + t // 2)[:, t % 2 * D:(t % 2 + 1) * D],
                                     learned_pt[:, t * P:(t + 1) * P], u_acc[:], start=True, stop=True)
                    if t % 2:
                        last.then_inc(lp_out, 1)

        @block.scalar
        def _(act):
            def high(it, x):
                kind, b = x
                n, b = n_chunk[x], b % B
                out = c_bank(n)
                act.wait_ge(chunk_done, CH.after(it, n))
                act.wait_ge(pair_cols_ready, it + (n // NC + 1))
                if kind == "q":
                    for hh in range(2):
                        last = act.activation(q_hi[:, b % 2, hh, :], out[:, hh * Q:(hh + 1) * Q], ACT.Identity,
                                              bias=cols[:, hh:hh + 1])
                elif kind in ("k0", "k1"):
                    hh = int(kind[1])
                    last = act.activation(k_hi[:, b % 2, hh, :], out, ACT.Identity, bias=cols[:, 2 + hh:3 + hh])
                else:
                    j = 2 * int(kind[1])
                    last = act.activation(v_hi[:, b % 2, j:j + 2, :], out.rearrange("p (j d) -> p j d", j=2), ACT.Copy)
                last.then_inc(chunk_high, 1)

            def high_mixed(it, x):
                if x[0] == "mix":
                    act.wait_ge(mix_done, MX.after(it, n_mix[x]))
                    act.activation(o_hi[:, x[1] % 2, :], m_bank[:, 0:Q], ACT.Copy).then_inc(mix_high, 1)

            def exp(it, g):
                act.wait_ge(max_ready, TILE1.after(it, g))
                act.wait_ge(turned, TILE1.after(it, g - NPB))
                act.wait_ge(learned_copied, TILE1.after(it, g - NPB))
                at = slice(g % NPB, g % NPB + 1)
                act.activation(probs[:, g % NPB, :], s_bank(g), ACT.Exp, bias=neg_max[:, at], scale=SC0,
                               accum_out=total[:, at]).then_inc(exp_ready, 1)
                b, hh, qt = g // 4, g // 2 % 2, g % 2
                act.activation(learned_e[:, at], lk_pair[:, b * QT + qt, hh:hh + 1], ACT.Exp, bias=neg_max[:, at],
                               scale=-1.0).then_inc(learned_e_ready, 1)

            def pt_high_part(it, g):
                u = g // 2
                act.wait_ge(turned, TILE1.after(it, g))
                if g % 2 == 0:
                    before = n_mix["mix", u - 2] if u >= 2 else n_mix["mix", u + 2 * B - 2] - NM
                    act.wait_ge(mix_done, MX.after(it, before))
                act.activation(pt_hi[:, u % 2, :, g % 2 * P:(g % 2 + 1) * P],
                               t_bank(g).rearrange("p (s q) -> p s q", s=ST), ACT.Copy).then_inc(pt_high, 1)

            def round_of(it, first=False, last=False):
                exp(it, 0)
                high(it, ("q", 1))
                exp(it, 1)
                if not first:
                    for x in LATE0:
                        high_mixed(it - 1, x)
                high(it, ("k0", 1))
                for g in range(N0):
                    if g + 2 < N0:
                        exp(it, g + 2)
                    for x in chunks_of(g):
                        if not (last and x[1] == B):
                            high(it, x)
                    pt_high_part(it, g)
                    for x in mixes_of(g):
                        high_mixed(it, x)

            act.nop().then_inc(exp_ready, N0)
            act.nop().then_inc(learned_e_ready, N0)
            with act.Fori(0, passes) as a:
                act.wait_ge(var_ready, a + 1)
                act.activation(root[:], var[:], ACT.Sqrt).then_inc(root_ready, 1)
                act.wait_ge(ln_loaded, (a + 1) * 16)
                for k in range(KD):
                    act.wait_ge(h_turned, a * KD + k + 1)
                    act.activation(h_full[:, k, :].rearrange("p (h n) -> p h n", h=2), sh.bank[k][:], ACT.Identity,
                                   scale=lncol[:, 0, k:k + 1], bias=lncol[:, 1, k:k + 1]).then_inc(h_scaled, 1)
                for x in EARLY0:
                    high(a * pairs, x)
                act.wait_ge(lk_done, a + 1)
                act.wait_ge(wq_lk_steps, a + 1)
                act.activation(lk_logit_t[:].rearrange("p (h n) -> p h n", h=2), sh.bank[0][0:H0], ACT.Identity,
                               bias=lk_bias[:], scale=-SC0).then_inc(lk_scaled, 1)
                act.wait_ge(lk_turned, a + 1)
                act.activation(lk_logit[:], sh.bank[1][:, 0, 0:XT * H0].rearrange("p (t h) -> p t h", t=XT), ACT.Copy)\
                   .then_inc(lk_logit_ready, 1)
                round_of(a * pairs, first=True)
                with act.Fori(1, pairs - 1) as hp:
                    round_of(a * pairs + hp)
                round_of(a * pairs + (pairs - 1), last=True)
                for x in LATE0:
                    high_mixed(a * pairs + (pairs - 1), x)
                act.wait_ge(lp_turned, a + 1)
                act.activation(learned_pt[:].rearrange("p (h n) -> p h n", h=2), sh.bank[0][0:H0 + 1], ACT.Copy)\
                   .then_inc(lp_copied, 1)

        @block.vector
        def _(dve):
            def low(it, x):
                kind, b = x
                n, b = n_chunk[x], b % B
                out = c_bank(n)
                dve.wait_ge(chunk_high, CH.after(it, n))
                if kind == "q":
                    for hh in range(2):
                        last = dve.scalar_tensor_tensor(q_lo[:, b % 2, hh, :], out[:, hh * Q:(hh + 1) * Q],
                                                        cols[:, hh:hh + 1], q_hi[:, b % 2, hh, :].bitcast(FP32),
                                                        ALU.add, ALU.subtract)
                elif kind in ("k0", "k1"):
                    hh = int(kind[1])
                    last = dve.scalar_tensor_tensor(k_lo[:, b % 2, hh, :], out, cols[:, 2 + hh:3 + hh],
                                                    k_hi[:, b % 2, hh, :].bitcast(FP32), ALU.add, ALU.subtract)
                else:
                    j = 2 * int(kind[1])
                    last = dve.tensor_tensor(v_lo[:, b % 2, j:j + 2, :], out.rearrange("p (j d) -> p j d", j=2),
                                             v_hi[:, b % 2, j:j + 2, :].bitcast(FP32), ALU.subtract)
                last.then_inc(chunk_ready, 1)

            def low_mixed(it, x):
                kind, b = x
                if kind == "mix":
                    dve.wait_ge(mix_high, MH.after(it, b))
                    last = dve.tensor_tensor(o_lo[:, b % 2, :], m_bank[:, 0:Q], o_hi[:, b % 2, :].bitcast(FP32), ALU.subtract)
                elif kind == "u":
                    dve.wait_ge(mix_done, MX.after(it, n_mix[x]))
                    last = dve.tensor_tensor(u_acc[:], m_bank[0:H0 + 1, 0:D], u_acc[:], ALU.add)
                else:
                    dve.wait_ge(mix_done, MX.after(it, n_mix[x]))
                    xb = sh.xs[:, b * QT:(b + 1) * QT, :]
                    last = dve.tensor_tensor(xb, m_bank.rearrange("p (t d) -> p t d", t=QT), xb, ALU.add)
                last.then_inc(mix_ready, 1)

            def tile_max(it, g):
                b, hh, qt = g // 4, g // 2 % 2, g % 2
                if g == 0:
                    dve.wait_ge(pair_logit_ready, it + 1)
                dve.wait_ge(learned_e_ready, TILE1.after(it, g - NPB))
                dve.wait_ge(scores_ready, TILE.after(it, g))
                dve.wait_ge(max_ready, TILE1.after(it, g - 2))
                dve.nop().then_inc(waits_taken_dve, 1)
                dve.tensor_tensor_reduce(out=junk[:, g % 2, :], in0=s_bank(g), in1=zeros[:].broadcast_to([P, S]),
                                         scale=-SC0, scalar=lk_pair[:, b * QT + qt, hh:hh + 1],
                                         op0=ALU.add, op1=ALU.min,
                                         accum_out=neg_max[:, g % NPB:g % NPB + 1]).then_inc(max_ready, 1)

            def inverse_sum(it, g):
                dve.wait_ge(learned_e_ready, TILE1.after(it, g))
                dve.wait_ge(learned_copied, TILE1.after(it, g - NPB))
                at = slice(g % NPB, g % NPB + 1)
                dve.tensor_tensor(denom[:, at], total[:, at], learned_e[:, at], ALU.add).then_inc(denom_steps, 1)
                dve.wait_ge(denom_steps, DEN.after(it, 2 * g))
                dve.reciprocal(denom[:, at], denom[:, at]).then_inc(denom_steps, 1)

            def pt_low_part(it, g):
                u = g // 2
                dve.wait_ge(pt_high, TILE.after(it, g))
                part = slice(g % 2 * P, (g % 2 + 1) * P)
                dve.tensor_tensor(pt_lo[:, u % 2, :, part], t_bank(g).rearrange("p (s q) -> p s q", s=ST),
                                  pt_hi[:, u % 2, :, part].bitcast(FP32), ALU.subtract).then_inc(pt_ready, 1)

            def round_of(it, first=False, last=False):
                tile_max(it, 0)
                tile_max(it, 1)
                low(it, ("q", 1))
                inverse_sum(it, 0)
                if not first:
                    low_mixed(it - 1, LATE0[0])
                inverse_sum(it, 1)
                low(it, ("k0", 1))
                tile_max(it, 2)
                for g in range(N0):
                    if g + 3 < N0:
                        tile_max(it, g + 3)
                    if g == 0 and not first:
                        low_mixed(it - 1, LATE0[1])
                    for x in chunks_of(g):
                        if not (last and x[1] == B):
                            low(it, x)
                    if g + 2 < N0:
                        inverse_sum(it, g + 2)
                    pt_low_part(it, g)
                    for x in mixes_of(g):
                        low_mixed(it, x)

            dve.nop().then_inc(chunk_ready, NC)
            dve.nop().then_inc(mix_ready, NM)
            dve.nop().then_inc(pt_ready, N0)
            dve.nop().then_inc(max_ready, N0)
            dve.nop().then_inc(xs_final, 1)
            dve.wait_ge(ones_ready, 2)
            with dve.Fori(0, passes) as a:
                dve.wait_ge(xs_final, a * 4 + 1)
                for t in range(XT):
                    dve.bn_stats(stats[:, t, :], sh.xs[:, t, :]).then_inc(stats_done, 1)
                dve.wait_ge(stats_done, (a + 1) * XT)
                dve.nop().then_inc(waits_taken_dve, 1)
                for t in range(XT):
                    dve.bn_aggr(mv[:, t, :], stats[:, t, :]).then_inc(mv_ready, 1)
                dve.wait_ge(mv_ready, (a + 1) * XT)
                dve.tensor_scalar(var[:], mv[:, :, 1], EPS0, None, ALU.add).then_inc(var_ready, 1)
                dve.wait_ge(root_ready, a + 1)
                inverse_root(dve, rstd_steps, a * NEWTON, rstd[:], var[:], root[:], newton[:])
                for t in range(XT):
                    dve.tensor_scalar(xn[:, t, :], sh.xs[:, t, :], mv[:, t, 0:1], rstd[:, t:t + 1],
                                      ALU.subtract, ALU.mult).then_inc(xn_ready, 1)
                for k in range(KD):
                    dve.wait_ge(h_scaled, a * KD + k + 1)
                    dve.tensor_copy(h_hi[:, k, :], h_full[:, k, :]).then_inc(h_high, 1)
                    dve.wait_ge(h_high, a * KD + k + 1)
                    dve.tensor_tensor(h_lo[:, k, :], h_full[:, k, :], h_hi[:, k, :].bitcast(FP32), ALU.subtract)\
                       .then_inc(h_ready, 1)
                dve.wait_ge(const_loaded, (a + 1) * 16)
                products = [(k, h) for k in range(KD) for h in range(H0)]
                for n, x in enumerate(EARLY0):
                    low(a * pairs, x)
                    if n == 0:
                        dve.wait_ge(wq_all_loaded, (a + 1) * 48)
                        dve.nop().then_inc(waits_taken_dve, 1)
                    for k, h in products[n::len(EARLY0)]:
                        part = slice(h * HD0, (h + 1) * HD0)
                        dve.tensor_tensor_reduce(out=wq_all[:, k, part], in0=wq_all[:, k, part], in1=lk_rows[:, part],
                                                 scale=1.0, scalar=0.0, op0=ALU.mult, op1=ALU.add,
                                                 accum_out=wq_lk[:, k, h:h + 1])
                dve.tensor_tensor_reduce(out=bq_lk[:, 0, :], in0=bq_lk[:, 0, :], in1=bq_lk[:, 1, :],
                                         scale=-SC0, scalar=0.0, op0=ALU.mult, op1=ALU.add,
                                         accum_out=lk_bias[:]).then_inc(wq_lk_steps, 1)
                round_of(a * pairs, first=True)
                with dve.Fori(1, pairs - 1) as hp:
                    round_of(a * pairs + hp)
                round_of(a * pairs + (pairs - 1), last=True)
                for x in LATE0:
                    low_mixed(a * pairs + (pairs - 1), x)
                for n in range(4):
                    dve.wait_ge(lp_out, a * 4 + n + 1)
                    dve.tensor_tensor(sh.xs[:, 2 * n:2 * n + 2, :], sh.one(4 + n).rearrange("p (t d) -> p t d", t=2),
                                      sh.xs[:, 2 * n:2 * n + 2, :], ALU.add).then_inc(xs_final, 1)


class Small:

    def __init__(self, name, heads, hd, kv_heads, keys, scale, mix_from, early_from, early_step):
        self.name, self.NH, self.HD, self.KVH, self.SK, self.scale = name, heads, hd, kv_heads, keys, scale
        self.UQ = heads // 4
        self.KH = 4 * kv_heads // heads
        self.KF = kv_heads * hd
        self.KK = -(-self.KF // P)
        self.KP = min(self.KF, P)
        self.W = 2 * D + 2 * self.KF
        self.GT = 8 * self.UQ
        self.KT = keys // P
        self.parts = 1 if keys <= 512 else 2
        self.PW = keys // self.parts
        self.NSB = 4 // self.parts
        self.ahead, self.max_ahead, self.exp_ahead = self.NSB, self.NSB, max(1, self.NSB - 1)
        self.NPB = 8 // self.parts
        VC = {32: 4, 16: 2}[heads]
        self.VC = VC
        self.v_chunks = [("v", c) for c in range(self.KT // VC)]
        self.early = [("x", 0), ("q", 0)] + [("k", (kk, c)) for kk in range(self.KK) for c in range(self.parts)]
        self.chunk_at = {}
        for i, x in enumerate(self.v_chunks):
            self.chunk_at.setdefault((3 if self.KT == 4 else 1) + i, []).append(x)
        for i, x in enumerate(self.early):
            self.chunk_at.setdefault(early_from + early_step * i, []).append(x)
        self.mixes = [(kind, j) for j in range(2 * self.UQ) for kind in ("av", "back")] + [("turn", 0), ("out", 0)]
        self.n_mix = {x: n for n, x in enumerate(self.mixes)}
        self.mix_at, self.take_at, self.late_at = {}, {}, {}
        last = 2 * self.UQ - 1
        for j in range(last):
            self.mix_at[4 * j + mix_from], self.mix_at[4 * j + 6] = ("av", j), ("back", j)
            self.take_at[4 * j + mix_from + 1], self.take_at[4 * j + 7] = ("av", j), ("back", j)
        for i, x in enumerate([("av", last), ("back", last), ("turn", 0), ("out", 0)]):
            self.late_at[i + mix_from - 4] = x
        self.CHUNK = Steps(len(self.v_chunks) + len(self.early), len(self.early))
        chunks = self.v_chunks + self.early
        self.n_chunk = {x: n for n, x in enumerate(chunks)}
        self.stack_dmas = 6 + (heads == 16)

    def chunk_count(self, it, x):
        return self.CHUNK.after(it, self.n_chunk[x])


L1 = Small("l1", 32, 8, 8, 512, 8.0 ** -0.5, 5, 6, 3)
L2 = Small("l2", 16, 16, 16, 512, 0.25, 5, 7, 2)
L3 = Small("l3", 16, 16, 16, 768, 1.0 / 16, 4, 9, 3)
ROWS = 65
MASKED = 1e30


def small_attention(nc, sh, L, k_src, weights, cols_dram, rows_dram, mask_dram, gate_dram, dest):
    HD, UQ, GT, KH, SK, KT, PW = L.HD, L.UQ, L.GT, L.KH, L.SK, L.KT, L.PW
    key_mask = L is not L1
    SCORE = Steps(GT, 1)
    TILE = Steps(GT, 4)
    TURN = Steps(GT * L.parts, L.NPB * L.parts)
    PARTS = Steps(GT * L.parts // 2, 1)
    MIX = Steps(len(L.mixes), len(L.mixes))
    USED = Steps(len(L.mixes), 1)
    halves = 2 * UQ
    src_hi, src_lo = k_src
    with ExitStack() as ctx:
        sb = lambda n, s, d=FP32: ctx.enter_context(nc.sbuf_tensor(L.name + n, s, d))
        sem = semaphores(nc, ctx, L.name)
        w_raw = sb("w_raw", [P, KD, L.W])
        w_hi, w_lo = sb("w_hi", [P, KD, L.W], FP32R), sb("w_lo", [P, KD, L.W], FP32R)
        cols = sb("cols", [P, 4])
        rows = sb("rows", [P, L.KF + D])
        gate = sb("gate", [P, 1])
        x_b = sb("x_b", [P, QT, D])
        src = [sb(f"src_{n}", [P, KD, S + Q], FP32R) for n in ("hi", "lo")]
        q_full = sb("q_full", [P, KD, Q])
        q_part = [sb(f"q_{n}", [P, KD, Q], FP32R) for n in ("hi", "lo")]
        k_part = [sb(f"k_{n}", [P, L.KK, SK], FP32R) for n in ("hi", "lo")]
        q_stack = [sb(f"q_stack{i}", [ROWS, 4, Q], FP32R) for i in range(2)]
        k_stack = [sb(f"k_stack{i}", [ROWS, KH, SK], FP32R) for i in range(2)]
        values = sb("values", [P, KT, L.KVH, 32])
        pt = sb("pt", [P, 2, 4, KT, P])
        probs = sb("probs", [P, L.NPB, SK])
        if key_mask:
            zeros = sb("zeros", [P, 1, 1])
            mask_raw = sb("mask_raw", [B, S], mask_dram.dtype)
            mask_bias = sb("mask_bias", [B, S])
            mask_row = sb("mask_row", [1, B, S])
        else:
            mask_in, mask = sb("mask_in", [P, QT, S]), sb("mask", [P, QT, S])
        neg_max = sb("neg_max", [P, L.NPB])
        av_sb = sb("av_sb", [P, P])
        inv = sb("inv", [P, 4])
        attn, result = (w_raw[:, i, 0:QT * D].rearrange("p (t d) -> p t d", t=QT) for i in range(2))
        attn_hi, attn_lo = sb("attn_hi", [P, KD, Q], FP32R), sb("attn_lo", [P, KD, Q], FP32R)
        q_rows = nc.dram_tensor(L.name + "_q_rows", (B, 2, D, Q), FP32).ap()
        k_rows = nc.dram_tensor(L.name + "_k_rows", (B, 2, L.KF, SK), FP32).ap()
        names = ("queries_stored keys_stored0 keys_stored1 weights_loaded small_loaded x_loaded src_loaded mask_loaded mask_copied mask_row_steps setup_done "
                 "w_high w_split cols_ready gate_ready chunk_done chunk_high chunk_used q_full_ready q_high "
                 "scores_ready max_ready exp_ready turned pt_copied_dve pt_copied_act mix_done mix_used "
                 "attn_high inv_ready result_ready stack_loaded0 stack_loaded1 waits_taken_dve waits_taken_sp")
        (queries_stored, keys_stored0, keys_stored1, weights_loaded, small_loaded, x_loaded, src_loaded, mask_loaded, mask_copied, mask_row_steps, setup_done,
         w_high, w_split, cols_ready, gate_ready, chunk_done, chunk_high, chunk_used, q_full_ready, q_high,
         scores_ready, max_ready, exp_ready, turned, pt_copied_dve, pt_copied_act, mix_done, mix_used,
         attn_high, inv_ready, result_ready, stack_loaded0, stack_loaded1, waits_taken_dve, waits_taken_sp) = map(sem, names.split())
        stack_loaded = (stack_loaded0, stack_loaded1)
        keys_stored = (keys_stored0, keys_stored1)
        pt_copied = (pt_copied_dve, pt_copied_act)
        NSM = 2 + (L is L2)
        STACKS_SET, SETUP = 6, 9
        block = ctx.enter_context(nc.Block())
        if L.parts == 1:
            s_bank = lambda g: sh.one(g % 4)[:, 0:PW].rearrange("p (c k) -> p c k", c=1)
        else:
            s_bank = lambda g: sh.bank[g % 2][:, :, 0:PW]
        m_bank = sh.one(7)
        bank_of = lambda x, start: sh.one(L.early.index(x)) if start else sh.one(6)
        part_of = lambda g, c: g * L.parts + c
        TP = PW // P
        pt_free = lambda it, g: MIX.after(it, L.n_mix["av", g // 4 - 2]) if g >= 8 else \
            MIX.after(it - 1, L.n_mix["av", g // 4 - 2 + halves])
        stack_count = lambda it, qd: (it * (UQ // 2) + qd // 2 + 1) * 16 * L.stack_dmas

        @block.sync
        def _(sp):
            def load_src(b):
                sp.dma_start(x_b[:], sh.xs[:, bass.ds(b * QT, QT), :]).then_inc(x_loaded, 16)
                for s_to, s_from in zip(src, (src_hi, src_lo)):
                    sp.dma_start(s_to[:, :, 0:S].bitcast(FP32), s_from[:, :, bass.ds(b * S, S)].bitcast(FP32)).then_inc(src_loaded, 16)

            def load_mask(b):
                sp.dma_start(mask_in[:], mask_dram[bass.ds(b, 1)].rearrange("o (t p) k -> p (o t) k", p=P))\
                  .then_inc(mask_loaded, 16)

            def store_queries(b):
                sp.wait_ge(chunk_used, L.chunk_count(b - 1, ("q", 0)))
                for n in range(2):
                    sp.dma_start(q_rows[bass.ds(b, 1), n].rearrange("o (k p) q -> p (o k) q", p=P), q_part[n][:].bitcast(FP32))\
                      .then_inc(queries_stored, 16)

            def store_keys(b, kk):
                sp.wait_ge(chunk_used, L.chunk_count(b - 1, ("k", (kk, L.parts - 1))))
                for n in range(2):
                    sp.dma_start(k_rows[bass.ds(b, 1), n, kk * L.KP:(kk + 1) * L.KP].rearrange("o p q -> (o p) q"),
                                 k_part[n][0:L.KP, kk, :].bitcast(FP32)).then_inc(keys_stored[kk], 16)

            def query_stack(b, qd):
                if qd == 0:
                    sp.wait_ge(queries_stored, (b + 1) * 32)
                for r in range(3):
                    sp.dma_start(q_stack[qd % 2][r * HD:(r + 1) * HD, :, :].bitcast(FP32),
                                 q_rows[bass.ds(b, 1), int(r == 2), qd * 4 * HD:(qd + 1) * 4 * HD, :]
                                 .rearrange("o (h d) q -> d (o h) q", d=HD)).then_inc(stack_loaded[qd % 2], 16)

            def key_stack(b, qd):
                if qd == 0:
                    sp.wait_ge(keys_stored[0], (b + 1) * 32)
                if L.KK == 2 and qd == UQ // 2:
                    sp.wait_ge(keys_stored[1], (b + 1) * 32)
                for r in range(3):
                    sp.dma_start(k_stack[qd % 2][r * HD:(r + 1) * HD, :, :].bitcast(FP32),
                                 k_rows[bass.ds(b, 1), int(r == 1), qd * KH * HD:(qd + 1) * KH * HD, :]
                                 .rearrange("o (h d) q -> d (o h) q", d=HD)).then_inc(stack_loaded[qd % 2], 16)
                if key_mask:
                    sp.dma_start(k_stack[qd % 2][ROWS - 1:ROWS, :, 0:S].bitcast(FP32),
                                 mask_row[:, bass.ds(b, 1), :].broadcast_to([1, KH, S])).then_inc(stack_loaded[qd % 2], 16)

            def round_of(b, last=False):
                for qd in range(1, UQ + 1):
                    if qd == UQ and last:
                        break
                    sp.wait_ge(scores_ready, SCORE.after(b, (qd - 1) * 8 - 1))
                    sp.nop().then_inc(waits_taken_sp, 1)
                    b_of, q_of = (b, qd) if qd < UQ else (b + 1, 0)
                    query_stack(b_of, q_of)
                    key_stack(b_of, q_of)
                    if qd == 1 and not last:
                        sp.wait_ge(chunk_used, L.chunk_count(b, L.v_chunks[-1]))
                        load_src(b + 1)
                        if not key_mask:
                            sp.wait_ge(mask_copied, b + 1)
                            load_mask(b + 1)
                    if qd == UQ - 1 and not last:
                        store_queries(b + 1)
                        for kk in range(L.KK):
                            store_keys(b + 1, kk)

            sp.dma_start(w_raw[:], weights.rearrange("(k p) w -> p k w", p=P)).then_inc(weights_loaded, 16)
            load_src(0)
            if key_mask:
                sp.dma_start(mask_raw[:], mask_dram).then_inc(mask_loaded, 16)
                sp.wait_ge(mask_row_steps, 1)
                sp.dma_start(mask_row[:], mask_bias[:]).then_inc(mask_loaded, 16)
            else:
                load_mask(0)
            store_queries(0)
            sp.wait_ge(setup_done, STACKS_SET)
            query_stack(0, 0)
            store_keys(0, 0)
            if key_mask:
                sp.wait_ge(mask_loaded, 32)
            key_stack(0, 0)
            if L.KK == 2:
                store_keys(0, 1)
            with sp.Fori(0, B - 1) as b:
                round_of(b)
            round_of(B - 1, last=True)

        @block.gpsimd
        def _(pool):
            for i in range(2):
                pool.memset(q_stack[i][:].bitcast(FP32), 0.0).then_inc(setup_done, 1)
                pool.memset(k_stack[i][:].bitcast(FP32), 0.0).then_inc(setup_done, 1)
            pool.wait_ge(setup_done, 4)
            if key_mask:
                for i in range(2):
                    pool.memset(q_stack[i][ROWS - 1:ROWS, :, :].bitcast(FP32), 1.0).then_inc(setup_done, 1)
            else:
                pool.nop().then_inc(setup_done, 2)
            pool.wait_ge(setup_done, STACKS_SET)
            pool.memset(values[:], 0.0).then_inc(setup_done, 1)
            pool.wait_ge(setup_done, STACKS_SET + 1)
            pool.memset(values[:, :, :, HD:HD + 1], 1.0).then_inc(setup_done, 1)
            pool.wait_ge(setup_done, STACKS_SET + 2)
            if key_mask:
                pool.memset(zeros[:], 0.0).then_inc(setup_done, 1)
            else:
                pool.nop().then_inc(setup_done, 1)

        @block.tensor
        def _(pe):
            def chunk(it, x, start=False):
                kind, c = x
                c_bank = bank_of(x, start)
                if not start:
                    pe.wait_ge(chunk_used, L.chunk_count(it, x) - 1)
                if kind == "x":
                    pe.wait_ge(x_loaded, (it + 2) * 16)
                    for k in range(KD):
                        for t in range(QT):
                            last = pe.transpose(c_bank[:, k * Q + t * P:k * Q + (t + 1) * P],
                                                x_b[:, t, k * P:(k + 1) * P], sh.ident[:])
                elif kind == "q":
                    pe.wait_ge(w_split, 4)
                    pe.wait_ge(chunk_used, L.chunk_count(it, ("x", 0)))
                    for half in range(KD):
                        for k in range(KD):
                            at = slice(half * P, (half + 1) * P)
                            last = mm3(pe, c_bank[:, half * Q:(half + 1) * Q], w_hi[:, k, at], w_lo[:, k, at],
                                       src[0][:, k, S:S + Q], src[1][:, k, S:S + Q], k == 0, k == KD - 1)
                elif kind == "k":
                    kk, part = c
                    pe.wait_ge(src_loaded, (it + 2) * 32)
                    at = slice(D + kk * P, D + kk * P + L.KP)
                    keys = slice(part * PW, (part + 1) * PW)
                    for k in range(KD):
                        last = mm3(pe, c_bank[0:L.KP, 0:PW], w_hi[:, k, at], w_lo[:, k, at],
                                   src[0][:, k, keys], src[1][:, k, keys], k == 0, k == KD - 1)
                else:
                    at = slice(D + L.KF, D + 2 * L.KF)
                    for t in range(L.VC):
                        keys = slice((c * L.VC + t) * P, (c * L.VC + t + 1) * P)
                        for k in range(KD):
                            last = mm3(pe, c_bank[:, t * L.KF:(t + 1) * L.KF], src[0][:, k, keys], src[1][:, k, keys],
                                       w_hi[:, k, at], w_lo[:, k, at], k == 0, k == KD - 1)
                last.then_inc(chunk_done, 1)

            def scores(it, g):
                qd, qt, h = g // 8, g // 4 % 2, g % 4
                if g % 8 == 0:
                    pe.wait_ge(stack_loaded[qd % 2], stack_count(it, qd))
                pe.wait_ge(max_ready, TILE.after(it, g - L.NSB))
                for c in range(L.parts):
                    last = pe.matmul(s_bank(g)[:, c, :], q_stack[qd % 2][:, h, qt * P:(qt + 1) * P],
                                     k_stack[qd % 2][:, h % KH, c * PW:(c + 1) * PW], start=True, stop=True)
                last.then_inc(scores_ready, 1)

            def turn(it, g):
                pe.wait_ge(exp_ready, TILE.after(it, g))
                for c in range(L.parts):
                    m = part_of(g, c)
                    pe.wait_ge(pt_copied[m % 2], PARTS.after(it, m // 2 - 1))
                    for s in range(TP):
                        last = pe.transpose(sh.one(4 + m % 2)[:, s * P:(s + 1) * P],
                                            probs[:, g % L.NPB, (c * TP + s) * P:(c * TP + s + 1) * P], sh.ident[:])
                    last.then_inc(turned, 1)

            def mix(it, x):
                kind, j = x
                pe.wait_ge(mix_used, USED.after(it, L.n_mix[x] - 1))
                if kind == "av":
                    for e in range(2):
                        pe.wait_ge(pt_copied[e], PARTS.after(it, part_of(4 * j + 3, L.parts - 1) // 2))
                    pe.wait_ge(chunk_used, L.chunk_count(it, L.v_chunks[-1]))
                    for s in range(KT):
                        for h in range(4):
                            head = (j // 2) * KH + h % KH
                            last = pe.matmul(m_bank[h * 32:(h + 1) * 32, 0:P], values[:, s, head, :],
                                             pt[:, j % 2, h, s, :], start=s == 0, stop=s == KT - 1)
                elif kind == "back":
                    last = pe.transpose(m_bank[:, 0:P], av_sb[:], sh.ident[:])
                elif kind == "turn":
                    for k in range(KD):
                        for t in range(QT):
                            last = pe.transpose(m_bank[:, k * Q + t * P:k * Q + (t + 1) * P],
                                                attn[:, t, k * P:(k + 1) * P], sh.ident[:])
                else:
                    at = slice(D + 2 * L.KF, 2 * D + 2 * L.KF)
                    for t in range(QT):
                        for k in range(KD):
                            last = mm3(pe, m_bank[:, t * D:(t + 1) * D],
                                       attn_hi[:, k, t * P:(t + 1) * P], attn_lo[:, k, t * P:(t + 1) * P],
                                       w_hi[:, k, at], w_lo[:, k, at], k == 0, k == KD - 1)
                last.then_inc(mix_done, 1)

            def round_of(it, first=False, last=False):
                for g in range(GT):
                    if g + L.ahead < GT:
                        scores(it, g + L.ahead)
                    elif not last:
                        scores(it + 1, g + L.ahead - GT)
                    for x in L.chunk_at.get(g, []):
                        if x in L.v_chunks or not last:
                            chunk(it, x)
                    turn(it, g)
                    if g in L.late_at and not first:
                        mix(it - 1, L.late_at[g])
                    if g in L.mix_at:
                        mix(it, L.mix_at[g])

            pe.nop().then_inc(turned, L.NPB * L.parts)
            pe.nop().then_inc(mix_done, len(L.mixes))
            pe.nop().then_inc(scores_ready, 1)
            for x in L.early:
                chunk(-1, x, start=True)
            pe.wait_ge(chunk_used, len(L.early))
            for g in range(L.ahead):
                scores(0, g)
            round_of(0, first=True)
            with pe.Fori(1, B - 1) as b:
                round_of(b)
            round_of(B - 1, last=True)
            for g in sorted(L.late_at):
                mix(B - 1, L.late_at[g])

        @block.scalar
        def _(act):
            def chunk(it, x, start=False):
                kind, c = x
                c_bank = bank_of(x, start)
                act.wait_ge(chunk_done, L.chunk_count(it, x))
                if kind == "x":
                    act.activation(src[0][:, :, S:S + Q], c_bank.rearrange("p (k q) -> p k q", k=KD), ACT.Copy)\
                       .then_inc(chunk_high, 1)
                elif kind == "q":
                    act.wait_ge(cols_ready, 1)
                    for half in range(KD):
                        last = act.activation(q_full[:, half, :], c_bank[:, half * Q:(half + 1) * Q], ACT.Identity,
                                              bias=cols[:, half:half + 1], scale=L.scale)
                    last.then_inc(chunk_high, 1)
                elif kind == "k":
                    kk, part = c
                    if not start:
                        act.wait_ge(keys_stored[kk], (it + 1) * 32)
                    act.activation(k_part[0][0:L.KP, kk, part * PW:(part + 1) * PW], c_bank[0:L.KP, 0:PW],
                                   ACT.Identity, bias=cols[0:L.KP, 2 + kk:3 + kk]).then_inc(chunk_high, 1)
                else:
                    act.nop().then_inc(chunk_high, 1)

            def exp(it, g):
                act.wait_ge(max_ready, TILE.after(it, g))
                to = probs[:, g % L.NPB, :].rearrange("p (c k) -> p c k", c=L.parts)
                at = neg_max[:, g % L.NPB:g % L.NPB + 1]
                act.activation(to, to, ACT.Exp, bias=at,
                               scale=-1.0).then_inc(exp_ready, 1)

            def pt_part(it, g):
                for c in range(L.parts):
                    m = part_of(g, c)
                    if m % 2 == 1:
                        act.wait_ge(turned, TURN.after(it, m))
                        act.wait_ge(mix_done, pt_free(it, g))
                        act.activation(pt[:, g // 4 % 2, g % 4, c * TP:(c + 1) * TP, :],
                                       sh.one(4 + m % 2)[:, 0:PW].rearrange("p (s q) -> p s q", s=TP), ACT.Copy)\
                           .then_inc(pt_copied_act, 1)

            def mix(it, x):
                kind, j = x
                if kind == "av":
                    act.wait_ge(mix_done, MIX.after(it, L.n_mix[x]))
                    act.activation(av_sb[:], m_bank[:, 0:P], ACT.Copy).then_inc(mix_used, 1)
                elif kind == "turn":
                    act.wait_ge(mix_done, MIX.after(it, L.n_mix[x]))
                    act.activation(attn_hi[:], m_bank.rearrange("p (k q) -> p k q", k=KD), ACT.Copy).then_inc(attn_high, 1)

            def round_of(it, first=False, last=False):
                for g in range(GT):
                    if g in L.take_at:
                        mix(it, L.take_at[g])
                    if g + L.exp_ahead < GT:
                        exp(it, g + L.exp_ahead)
                    elif not last:
                        exp(it + 1, g + L.exp_ahead - GT)
                    for x in L.chunk_at.get(g, []):
                        if x in L.v_chunks or not last:
                            chunk(it, x)
                    pt_part(it, g)
                    if g in L.late_at and not first:
                        mix(it - 1, L.late_at[g])

            act.nop().then_inc(exp_ready, 4)
            act.nop().then_inc(pt_copied_act, 1)
            act.dma_start(cols[:], cols_dram).then_inc(small_loaded, 16)
            act.dma_start(rows[:], rows_dram.partition_broadcast(P)).then_inc(small_loaded, 16)
            if L is L2:
                act.dma_start(gate[:], gate_dram.partition_broadcast(P)).then_inc(small_loaded, 16)
            act.wait_ge(weights_loaded, 16)
            for k in range(KD):
                for n in range(2):
                    part = slice(n * (L.W // 2), (n + 1) * (L.W // 2))
                    act.activation(w_hi[:, k, part], w_raw[:, k, part], ACT.Copy).then_inc(w_high, 1)
            if L is L2:
                act.wait_ge(small_loaded, NSM * 16)
                act.activation(gate[:], gate[:], ACT.Tanh).then_inc(gate_ready, 1)
            for x in L.early:
                chunk(-1, x, start=True)
            for g in range(L.exp_ahead):
                exp(0, g)
            round_of(0, first=True)
            with act.Fori(1, B - 1) as b:
                round_of(b)
            round_of(B - 1, last=True)
            for g in sorted(L.late_at):
                mix(B - 1, L.late_at[g])

        @block.vector
        def _(dve):
            def chunk(it, x, start=False):
                kind, c = x
                n = L.chunk_count(it, x)
                c_bank = bank_of(x, start)
                dve.wait_ge(chunk_high, n)
                if kind == "x":
                    dve.tensor_tensor(src[1][:, :, S:S + Q], c_bank.rearrange("p (k q) -> p k q", k=KD),
                                      src[0][:, :, S:S + Q].bitcast(FP32), ALU.subtract).then_inc(chunk_used, 1)
                elif kind == "q":
                    if not start:
                        dve.wait_ge(queries_stored, (it + 1) * 32)
                    dve.tensor_copy(q_part[0][:], q_full[:]).then_inc(q_high, 1)
                    dve.wait_ge(q_high, it + 2)
                    dve.tensor_tensor(q_part[1][:], q_full[:], q_part[0][:].bitcast(FP32), ALU.subtract).then_inc(chunk_used, 1)
                elif kind == "k":
                    kk, part = c
                    keys = slice(part * PW, (part + 1) * PW)
                    dve.scalar_tensor_tensor(k_part[1][0:L.KP, kk, keys], c_bank[0:L.KP, 0:PW], cols[0:L.KP, 2 + kk:3 + kk],
                                             k_part[0][0:L.KP, kk, keys].bitcast(FP32), ALU.add, ALU.subtract)\
                       .then_inc(chunk_used, 1)
                else:
                    for t in range(L.VC):
                        last = dve.tensor_tensor(
                            values[:, c * L.VC + t, :, 0:HD],
                            c_bank[:, t * L.KF:(t + 1) * L.KF].rearrange("p (h d) -> p h d", d=HD),
                            rows[:, 0:L.KF].rearrange("p (h d) -> p h d", d=HD), ALU.add)
                    last.then_inc(chunk_used, 1)

            def tile_max(it, g):
                dve.wait_ge(scores_ready, SCORE.after(it, g))
                dve.wait_ge(turned, TURN.after(it, part_of(g - L.NPB, L.parts - 1)))
                dve.nop().then_inc(waits_taken_dve, 1)
                qt = g // 4 % 2
                dve.tensor_tensor_reduce(out=probs[:, g % L.NPB, :].rearrange("p (c k) -> p c k", c=L.parts), in0=s_bank(g),
                                         in1=zeros[:].broadcast_to([P, L.parts, PW]) if key_mask else mask[:, qt:qt + 1, :], scale=-1.0, scalar=3e38,
                                         op0=ALU.add, op1=ALU.min, accum_out=neg_max[:, g % L.NPB:g % L.NPB + 1])\
                   .then_inc(max_ready, 1)

            def pt_part(it, g):
                for c in range(L.parts):
                    m = part_of(g, c)
                    if m % 2 == 0:
                        dve.wait_ge(turned, TURN.after(it, m))
                        dve.wait_ge(mix_done, pt_free(it, g))
                        dve.tensor_copy(pt[:, g // 4 % 2, g % 4, c * TP:(c + 1) * TP, :],
                                        sh.one(4 + m % 2)[:, 0:PW].rearrange("p (s q) -> p s q", s=TP))\
                           .then_inc(pt_copied_dve, 1)

            def mix(it, x):
                kind, j = x
                n = MIX.after(it, L.n_mix[x])
                if kind == "back":
                    dve.wait_ge(mix_done, n)
                    by_head = m_bank[:, 0:P].rearrange("p (h d) -> p h d", h=4)
                    dve.reciprocal(inv[:], by_head[:, :, HD]).then_inc(inv_ready, 1)
                    dve.wait_ge(inv_ready, it * halves + j + 1)
                    at = (j // 2) * 4 * HD
                    dve.tensor_tensor(attn[:, j % 2, at:at + 4 * HD].rearrange("p (h d) -> p h d", h=4), by_head[:, :, 0:HD],
                                      inv[:].rearrange("p (h o) -> p h o", o=1).broadcast_to([P, 4, HD]), ALU.mult)\
                       .then_inc(mix_used, 1)
                elif kind == "turn":
                    dve.wait_ge(attn_high, it + 1)
                    dve.tensor_tensor(attn_lo[:], m_bank.rearrange("p (k q) -> p k q", k=KD), attn_hi[:].bitcast(FP32),
                                      ALU.subtract).then_inc(mix_used, 1)
                elif kind == "out":
                    dve.wait_ge(mix_done, n)
                    for t in range(QT):
                        last = dve.scalar_tensor_tensor(result[:, t, :], m_bank[:, t * D:(t + 1) * D], gate[:],
                                                        rows[:, L.KF:L.KF + D], ALU.mult, ALU.add)
                    last.then_inc(mix_used, 1)
                    dve.wait_ge(mix_used, USED.after(it, L.n_mix[x]))
                    at = bass.ds(it * QT, QT)
                    dve.tensor_tensor(dest[:, at, :], result, sh.xs[:, at, :], ALU.add).then_inc(result_ready, 1)

            def next_mask(it):
                dve.wait_ge(mask_loaded, (it + 1) * 16)
                dve.wait_ge(max_ready, TILE.after(it, -1))
                dve.tensor_copy(mask[:], mask_in[:]).then_inc(mask_copied, 1)
                dve.wait_ge(mask_copied, it + 1)

            def round_of(it, first=False, last=False):
                for g in range(GT):
                    if g + L.max_ahead < GT:
                        tile_max(it, g + L.max_ahead)
                    elif not last:
                        if g + L.max_ahead == GT and not key_mask:
                            next_mask(it + 1)
                        tile_max(it + 1, g + L.max_ahead - GT)
                    for x in L.chunk_at.get(g, []):
                        if x in L.v_chunks or not last:
                            chunk(it, x)
                    pt_part(it, g)
                    if g in L.late_at and not first:
                        mix(it - 1, L.late_at[g])
                    if g in L.take_at:
                        mix(it, L.take_at[g])

            dve.nop().then_inc(max_ready, 4)
            dve.nop().then_inc(pt_copied_dve, 1)
            dve.nop().then_inc(mix_used, 1)
            for k in range(KD):
                for n in range(2):
                    dve.wait_ge(w_high, 2 * k + n + 1)
                    part = slice(n * (L.W // 2), (n + 1) * (L.W // 2))
                    dve.tensor_tensor(w_lo[:, k, part], w_raw[:, k, part], w_hi[:, k, part].bitcast(FP32), ALU.subtract)\
                       .then_inc(w_split, 1)
            dve.wait_ge(small_loaded, NSM * 16)
            if L is not L2:
                dve.memset(gate[:], 1.0).then_inc(gate_ready, 1)
            dve.wait_ge(gate_ready, 1)
            dve.tensor_scalar(cols[:, 0:2], cols[:, 0:2], L.scale, None, ALU.mult).then_inc(cols_ready, 1)
            for x in L.early:
                chunk(-1, x, start=True)
                if x[0] == "x" and key_mask:
                    dve.wait_ge(mask_loaded, 16)
                    dve.tensor_scalar(mask_bias[:], mask_raw[:], 0.0, -MASKED, ALU.is_equal, ALU.mult).then_inc(mask_row_steps, 1)
            dve.wait_ge(setup_done, SETUP)
            if not key_mask:
                next_mask(0)
            for g in range(L.max_ahead):
                tile_max(0, g)
            round_of(0, first=True)
            with dve.Fori(1, B - 1) as b:
                round_of(b)
            round_of(B - 1, last=True)
            for g in sorted(L.late_at):
                mix(B - 1, L.late_at[g])


def token_stats(dve, tokens, tiles, stats, mv, stats_done, mv_ready):
    for t in tiles:
        dve.bn_stats(stats[:, t, :], tokens[:, t, :]).then_inc(stats_done, 1)
    for i, t in enumerate(tiles):
        dve.wait_ge(stats_done, i + 1)
        dve.bn_aggr(mv[:, t, :], stats[:, t, :]).then_inc(mv_ready, 1)


def norm_stream_and_context(nc, sh, rows_dram, ctx_dram, cols_dram, out_hi, out_lo):
    CT = C // P
    with ExitStack() as ctx:
        sb = lambda n, s, d=FP32: ctx.enter_context(nc.sbuf_tensor("n2" + n, s, d))
        sem = semaphores(nc, ctx, "n2")
        rows = sb("rows", [P, 2 * D])
        x_stats, x_mv = sb("x_stats", [P, XT, 6]), sb("x_mv", [P, XT, 2])
        x_var, x_root, x_rstd, x_newton = (sb("x_" + n, [P, XT]) for n in ("var", "root", "rstd", "newton"))
        (rows_loaded, x_stats_done, x_mv_ready, x_var_ready, x_root_ready, x_rstd_steps, x_normed, x_scaled_pool,
         x_scaled_dve) = map(sem, ("rows_loaded x_stats_done x_mv_ready x_var_ready x_root_ready x_rstd_steps x_normed "
                                   "x_scaled_pool x_scaled_dve").split())
        ctok = sb("ctok", [P, CT, D])
        cols = sb("cols", [P, 2, KD])
        full = sb("full", [P, 2, S])
        stats, mv = sb("stats", [P, CT, 6]), sb("mv", [P, CT, 2])
        var, root, rstd, newton = (sb(n, [P, CT]) for n in ("var", "root", "rstd", "newton"))
        cols_loaded, stats_done, mv_ready, var_ready, root_ready, rstd_steps, normed, turned, scaled, high, split = map(
            sem, "cols_loaded stats_done mv_ready var_ready root_ready rstd_steps normed turned scaled high split".split())
        ctx_loaded = [sem(f"ctx_loaded{b}") for b in range(B)]
        block = ctx.enter_context(nc.Block())

        @block.sync
        def _(sp):
            sp.dma_start(rows[:], rows_dram.partition_broadcast(P)).then_inc(rows_loaded, 16)
            for b in range(B):
                sp.dma_start(ctok[:, b * ST:(b + 1) * ST, :],
                             ctx_dram[b * S:(b + 1) * S, :].rearrange("(t p) d -> p t d", p=P)).then_inc(ctx_loaded[b], 16)
            sp.dma_start(cols[:], cols_dram).then_inc(cols_loaded, 16)

        @block.tensor
        def _(pe):
            for n in range(B * KD):
                b, k = n // KD, n % KD
                pe.wait_ge(normed, (b + 1) * ST)
                for t in range(ST):
                    last = pe.transpose(sh.one(n)[:, t * P:(t + 1) * P],
                                        ctok[:, b * ST + t, k * P:(k + 1) * P], sh.ident[:])
                last.then_inc(turned, 1)

        @block.scalar
        def _(act):
            act.wait_ge(x_var_ready, 1)
            act.activation(x_root[:], x_var[:], ACT.Sqrt).then_inc(x_root_ready, 1)
            for b in range(B):
                at = slice(b * ST, (b + 1) * ST)
                act.wait_ge(var_ready, b + 1)
                act.activation(root[:, at], var[:, at], ACT.Sqrt).then_inc(root_ready, 1)
            act.wait_ge(cols_loaded, 16)
            for n in range(B * KD):
                act.wait_ge(turned, n + 1)
                if n >= 2:
                    act.wait_ge(split, n - 1)
                k = n % KD
                act.activation(full[:, n % 2, :], sh.one(n), ACT.Identity, scale=cols[:, 0, k:k + 1],
                               bias=cols[:, 1, k:k + 1]).then_inc(scaled, 1)

        @block.gpsimd
        def _(pool):
            pool.wait_ge(rows_loaded, 16)
            for t in range(1, XT, 2):
                pool.wait_ge(x_normed, t + 1)
                pool.tensor_tensor(sh.xs[:, t, :], sh.xs[:, t, :], rows[:, 0:D], ALU.mult).then_inc(x_scaled_pool, 1)
                pool.wait_ge(x_scaled_pool, t // 2 + 1)
                pool.tensor_tensor(sh.xs[:, t, :], sh.xs[:, t, :], rows[:, D:2 * D], ALU.add)
            for n in range(B * KD):
                b, k = n // KD, n % KD
                pool.wait_ge(high, n + 1)
                pool.tensor_tensor(out_lo[:, k, b * S:(b + 1) * S], full[:, n % 2, :],
                                   out_hi[:, k, b * S:(b + 1) * S].bitcast(FP32), ALU.subtract).then_inc(split, 1)

        @block.vector
        def _(dve):
            token_stats(dve, sh.xs, range(XT), x_stats, x_mv, x_stats_done, x_mv_ready)
            dve.wait_ge(x_mv_ready, XT)
            dve.tensor_scalar(x_var[:], x_mv[:, :, 1], 1e-6, None, ALU.add).then_inc(x_var_ready, 1)
            dve.wait_ge(x_root_ready, 1)
            inverse_root(dve, x_rstd_steps, 0, x_rstd[:], x_var[:], x_root[:], x_newton[:])
            for t in range(XT):
                dve.tensor_scalar(sh.xs[:, t, :], sh.xs[:, t, :], x_mv[:, t, 0:1], x_rstd[:, t:t + 1],
                                  ALU.subtract, ALU.mult).then_inc(x_normed, 1)
            for b in range(B):
                dve.wait_ge(ctx_loaded[b], 16)
                for t in range(b * ST, (b + 1) * ST):
                    dve.bn_stats(stats[:, t, :], ctok[:, t, :]).then_inc(stats_done, 1)
                for t in range(b * ST, (b + 1) * ST):
                    dve.wait_ge(stats_done, t + 1)
                    dve.bn_aggr(mv[:, t, :], stats[:, t, :]).then_inc(mv_ready, 1)
                at = slice(b * ST, (b + 1) * ST)
                dve.wait_ge(mv_ready, (b + 1) * ST)
                dve.tensor_scalar(var[:, at], mv[:, at, 1], 1e-5, None, ALU.add).then_inc(var_ready, 1)
            for b in range(B):
                at = slice(b * ST, (b + 1) * ST)
                dve.wait_ge(root_ready, b + 1)
                inverse_root(dve, rstd_steps, b * NEWTON, rstd[:, at], var[:, at], root[:, at], newton[:, at])
                for t in range(b * ST, (b + 1) * ST):
                    dve.tensor_scalar(ctok[:, t, :], ctok[:, t, :], mv[:, t, 0:1], rstd[:, t:t + 1],
                                      ALU.subtract, ALU.mult).then_inc(normed, 1)
            for n in range(B * KD):
                b, k = n // KD, n % KD
                dve.wait_ge(scaled, n + 1)
                dve.tensor_copy(out_hi[:, k, b * S:(b + 1) * S], full[:, n % 2, :]).then_inc(high, 1)
            dve.wait_ge(rows_loaded, 16)
            dve.wait_ge(x_normed, XT)
            for t in range(0, XT, 2):
                dve.tensor_tensor(sh.xs[:, t, :], sh.xs[:, t, :], rows[:, 0:D], ALU.mult).then_inc(x_scaled_dve, 1)
            for t in range(0, XT, 2):
                dve.wait_ge(x_scaled_dve, t // 2 + 1)
                dve.tensor_tensor(sh.xs[:, t, :], sh.xs[:, t, :], rows[:, D:2 * D], ALU.add)


FF = 4 * D
FT = FF // P


def mlp(nc, sh, name, tokens, gelu, rms, eps, w1_dram, w2_dram, cols_dram, b2_dram, out_dram=None):
    HT = T // 2
    with ExitStack() as ctx:
        sb = lambda n, s, d=FP32: ctx.enter_context(nc.sbuf_tensor(name + n, s, d))
        sem = semaphores(nc, ctx, name)
        w1_raw, w2_raw = sb("w1_raw", [P, KD, FF]), sb("w2_raw", [P, FT, D])
        w1 = [sb(f"w1_{n}", [P, KD, FF], FP32R) for n in ("hi", "lo")]
        w2 = [sb(f"w2_{n}", [P, FT, D], FP32R) for n in ("hi", "lo")]
        cols = sb("cols", [P, FT + 2 * KD])
        b2 = sb("b2", [P, D])
        stats, mv, sq = sb("stats", [P, XT, 6]), sb("mv", [P, XT, 2]), sb("sq", [P, XT])
        var, root, rstd, newton = (sb(n, [P, XT]) for n in ("var", "root", "rstd", "newton"))
        xn = sb("xn", [P, XT, D])
        h_full = sb("h_full", [P, 2, HT])
        h = [sb(f"h_{n}", [P, KD, T], FP32R) for n in ("hi", "lo")]
        a_full = sb("a_full", [P, 2, HT])
        a = [sb(f"a_{n}", [P, FT, HT], FP32R) for n in ("hi", "lo")]
        names = ("w1_loaded w2_loaded small_loaded w_high w_split stats_done mv_ready var_steps var_ready root_ready rstd_steps normed "
                 "turned scaled h_high h_split up_done gelu_done a_high a_split down_done added out_stored")
        (w1_loaded, w2_loaded, small_loaded, w_high, w_split, stats_done, mv_ready, var_steps, var_ready, root_ready, rstd_steps, normed,
         turned, scaled, h_high, h_split, up_done, gelu_done, a_high, a_split, down_done, added, out_stored) = map(sem, names.split())
        block = ctx.enter_context(nc.Block())

        @block.sync
        def _(sp):
            sp.dma_start(w1_raw[:], w1_dram.rearrange("(k p) f -> p k f", p=P)).then_inc(w1_loaded, 16)
            sp.dma_start(w2_raw[:], w2_dram.rearrange("(k p) f -> p k f", p=P)).then_inc(w2_loaded, 16)
            sp.dma_start(cols[:], cols_dram).then_inc(small_loaded, 16)
            sp.dma_start(b2[:], b2_dram.partition_broadcast(P)).then_inc(small_loaded, 16)
            if out_dram is not None:
                for t in range(0, XT, 2):
                    sp.wait_ge(added, t + 2)
                    sp.dma_start(out_dram[t * P:(t + 2) * P, :].rearrange("(t p) d -> p t d", p=P), sh.xs[:, t:t + 2, :])\
                      .then_inc(out_stored, 16)
                sp.wait_ge(out_stored, 16 * XT // 2)

        raw = [w1_raw[:, i // 2, i % 2 * 512:(i % 2 + 1) * 512] for i in range(4)] + \
              [w2_raw[:, 2 * i:2 * i + 2, :] for i in range(4)]
        parts = [[w1[j][:, i // 2, i % 2 * 512:(i % 2 + 1) * 512] for i in range(4)] +
                 [w2[j][:, 2 * i:2 * i + 2, :] for i in range(4)] for j in range(2)]

        @block.gpsimd
        def _(pool):
            for i in range(8):
                pool.wait_ge(w_high, i + 1)
                pool.tensor_tensor(parts[1][i], raw[i], parts[0][i].bitcast(FP32), ALU.subtract).then_inc(w_split, 1)

        @block.tensor
        def _(pe):
            for n in range(4):
                pe.wait_ge(normed, (n // 2 + 1) * 4)
                for t in range(4):
                    last = pe.transpose(sh.one(n)[:, t * P:(t + 1) * P],
                                        xn[:, n // 2 * 4 + t, n % 2 * P:(n % 2 + 1) * P], sh.ident[:])
                last.then_inc(turned, 1)
            pe.wait_ge(w_split, 4)

            def up(half, f):
                n = half * FT + f
                if n >= 4:
                    pe.wait_ge(gelu_done, n - 3)
                pe.wait_ge(h_split, (half + 1) * KD)
                for k in range(KD):
                    last = mm3(pe, sh.one(4 + n % 4), w1[0][:, k, f * P:(f + 1) * P], w1[1][:, k, f * P:(f + 1) * P],
                               h[0][:, k, half * HT:(half + 1) * HT], h[1][:, k, half * HT:(half + 1) * HT], k == 0, k == KD - 1)
                last.then_inc(up_done, 1)

            def down(half, t):
                n = half * 4 + t
                if n >= 4:
                    pe.wait_ge(added, n - 3)
                if n == 0:
                    pe.wait_ge(w_split, 8)
                    pe.wait_ge(h_split, 4)
                for f in range(FT):
                    if t == 0:
                        pe.wait_ge(a_split, half * FT + f + 1)
                    last = mm3(pe, sh.one(n % 4)[:, 0:D], a[0][:, f, t * P:(t + 1) * P], a[1][:, f, t * P:(t + 1) * P],
                               w2[0][:, f, :], w2[1][:, f, :], f == 0, f == FT - 1)
                last.then_inc(down_done, 1)

            for half in range(2):
                for f in range(FT):
                    up(half, f)
                for t in range(4):
                    down(half, t)

        @block.scalar
        def _(act):
            act.wait_ge(var_ready, 1)
            act.activation(root[:], var[:], ACT.Sqrt).then_inc(root_ready, 1)
            for i in range(4):
                act.wait_ge(w1_loaded, 16)
                act.activation(parts[0][i], raw[i], ACT.Copy).then_inc(w_high, 1)
            act.wait_ge(small_loaded, 32)
            for n in range(4):
                act.wait_ge(turned, n + 1)
                if n >= 2:
                    act.wait_ge(h_split, n - 1)
                k = n % 2
                act.activation(h_full[:, n % 2, :], sh.one(n), ACT.Identity, scale=cols[:, FT + k:FT + k + 1],
                               bias=cols[:, FT + KD + k:FT + KD + k + 1]).then_inc(scaled, 1)
            for i in range(4, 8):
                act.wait_ge(w2_loaded, 16)
                act.activation(parts[0][i], raw[i], ACT.Copy).then_inc(w_high, 1)
            for n in range(2 * FT):
                act.wait_ge(up_done, n + 1)
                if n >= 2:
                    act.wait_ge(a_split, n - 1)
                f = n % FT
                act.activation(a_full[:, n % 2, :], sh.one(4 + n % 4), gelu, bias=cols[:, f:f + 1]).then_inc(gelu_done, 1)

        @block.vector
        def _(dve):
            if rms:
                for t in range(XT):
                    dve.tensor_tensor_reduce(out=xn[:, t, :], in0=tokens[:, t, :], in1=tokens[:, t, :], scale=1.0 / D,
                                             scalar=0.0, op0=ALU.mult, op1=ALU.add, accum_out=sq[:, t:t + 1])\
                       .then_inc(var_steps, 1)
                dve.wait_ge(var_steps, XT)
                dve.tensor_scalar(var[:], sq[:], eps, None, ALU.add).then_inc(var_ready, 1)
            else:
                token_stats(dve, tokens, range(XT), stats, mv, stats_done, mv_ready)
                dve.wait_ge(mv_ready, XT)
                dve.tensor_scalar(var[:], mv[:, :, 1], eps, None, ALU.add).then_inc(var_ready, 1)
            dve.wait_ge(root_ready, 1)
            inverse_root(dve, rstd_steps, 0, rstd[:], var[:], root[:], newton[:])
            for t in range(XT):
                if rms:
                    dve.tensor_scalar(xn[:, t, :], tokens[:, t, :], rstd[:, t:t + 1], None, ALU.mult).then_inc(normed, 1)
                else:
                    dve.tensor_scalar(xn[:, t, :], tokens[:, t, :], mv[:, t, 0:1], rstd[:, t:t + 1],
                                      ALU.subtract, ALU.mult).then_inc(normed, 1)
            for n in range(4):
                half, k = n // 2, n % 2
                to = [h[j][:, k, half * HT:(half + 1) * HT] for j in range(2)]
                dve.wait_ge(scaled, n + 1)
                dve.tensor_copy(to[0], h_full[:, n % 2, :]).then_inc(h_high, 1)
                dve.wait_ge(h_high, n + 1)
                dve.tensor_tensor(to[1], h_full[:, n % 2, :], to[0].bitcast(FP32), ALU.subtract).then_inc(h_split, 1)
            dve.wait_ge(small_loaded, 32)
            for t in range(XT):
                dve.tensor_tensor(sh.xs[:, t, :], sh.xs[:, t, :], b2[:], ALU.add).then_inc(var_steps, 1)
            for half in range(2):
                for f in range(FT):
                    n = half * FT + f
                    dve.wait_ge(gelu_done, n + 1)
                    if half:
                        dve.wait_ge(down_done, 4)
                    dve.tensor_copy(a[0][:, f, :], a_full[:, n % 2, :]).then_inc(a_high, 1)
                    dve.wait_ge(a_high, n + 1)
                    dve.tensor_tensor(a[1][:, f, :], a_full[:, n % 2, :], a[0][:, f, :].bitcast(FP32), ALU.subtract)\
                       .then_inc(a_split, 1)
                for t in range(4):
                    n = half * 4 + t
                    dve.wait_ge(down_done, n + 1)
                    dve.wait_ge(var_steps, (XT if rms else 0) + n + 1)
                    dve.tensor_tensor(sh.xs[:, n, :], sh.one(n % 4)[:, 0:D], sh.xs[:, n, :], ALU.add).then_inc(added, 1)


def layer0_packs(get):
    packs = np.zeros((2 * NP0 + 1, P, PACK_W), np.float32)
    for a in range(2):
        w = {n: get(f"w{n}{a + 1}") for n in "qkvo"}
        small = [get(f"bq{a + 1}"), get(f"bk{a + 1}"), get(f"bias_v{a + 1}").reshape(-1), get(f"bv{a + 1}")]
        for hp in range(NP0):
            to, heads = packs[a * NP0 + hp], slice(hp * 2 * HD0, (hp + 1) * 2 * HD0)
            for n, name in enumerate("qkv"):
                to[:, 2 * n * D:2 * (n + 1) * D] = w[name][:, heads].reshape(KD, P, D).transpose(1, 0, 2).reshape(P, -1)
            to[:, 6 * D:8 * D] = w["o"][heads].reshape(2, P, D).transpose(1, 0, 2).reshape(P, -1)
            for n, v in enumerate(small):
                to[:, 8 * D + 2 * n:8 * D + 2 * n + 2] = v[heads].reshape(2, P).T
            for hh in range(2):
                to[:, COL_SEL + hh * (H0 + 1) + 2 * hp + hh] = 1.0
    return packs


def layer0_consts(get):
    ln = np.stack([np.stack([get(f"ln{a}_{n}").reshape(KD, P).T for n in ("scale", "offset")], 1) for a in (1, 2)])
    u = np.zeros((2, H0 + 1, D), np.float32)
    for a in (1, 2):
        u[a - 1, H0] = get(f"bo{a}")
    wq = np.stack([get("wq1"), get("wq2")])
    lk = np.stack([get(f"bias_k{a}").reshape(-1) for a in (1, 2)])
    bq_lk = np.stack([np.stack([get(f"bq{a}").reshape(H0, HD0), get(f"bias_k{a}").reshape(H0, HD0)], 1) for a in (1, 2)])
    return np.ascontiguousarray(ln), u, wq, lk, bq_lk


def by_partition(*vectors):
    return np.concatenate([v.reshape(-1, P).T for v in vectors], 1)


def small_columns(bq, bk):
    cols = np.zeros((P, 4), np.float32)
    cols[:, 0:2] = by_partition(bq)
    if bk.size < P:
        cols[:bk.size, 2] = bk
    else:
        cols[:, 2:4] = by_partition(bk)
    return cols


def layouts(get):
    l0 = lambda n: get("L0_xattn_" + n)
    l1 = lambda n: get("L1_xattn_" + n)
    l2 = lambda n: get("L2_xattn_" + n)
    l3 = lambda n: get("L3_xattn_" + n)
    zero = np.zeros(D, np.float32)
    side = lambda *w: np.concatenate(w, 1)
    row = lambda *v: np.concatenate(v)[None]
    ln, u, wq, lk, bq_lk = layer0_consts(l0)
    a = dict(x=get("x").reshape(T, D), ctx=get("ctx_2048").reshape(C, D),
             packs=layer0_packs(l0), ln=ln, u=u, wq=wq, lk=lk, bq_lk=bq_lk,
             fc1=l0("w_fc1"), fc2=l0("w_fc2"), fc2_bias=row(l0("b_fc2")),
             fc_cols=by_partition(l0("b_fc1"), l0("ln_mlp_scale"), l0("ln_mlp_offset")),
             l1_w=side(l1("Wq"), l1("Wk"), l1("Wv"), l1("Wo")), l1_cols=small_columns(l1("bq"), l1("bk")),
             l1_rows=row(l1("bv"), l1("bo")), l1_mask=get("mask_Bx1xSxS2_ff0").reshape(B, Q, S),
             l1_norm=row(l1("gamma"), l1("beta")),
             l2_w=side(l2("Wq").T, l2("Wk").T, l2("Wv").T, l2("Wo").T), l2_cols=small_columns(zero, zero),
             l2_rows=row(zero, zero), l2_mask=get("mask_BxS2_bf1").view(np.uint8), l2_gate=l2("gate")[None],
             l2_norm=np.stack([by_partition(l2("ln_gamma")), by_partition(l2("ln_beta"))], 1),
             l3_w=side(l3("q_w"), l3("kv_w")[:, 0::2], l3("kv_w")[:, 1::2], l3("out_w")),
             l3_cols=small_columns(l3("q_b"), l3("kv_b")[0::2]), l3_rows=row(l3("kv_b")[1::2], l3("out_b")),
             l3_mask=get("mask_BxS2_ik0"),
             mlp1=l3("mlp_w1"), mlp2=l3("mlp_w2"), mlp2_bias=row(l3("mlp_b2")),
             mlp_cols=by_partition(l3("mlp_b1"), l3("postnorm_w"), zero))
    return {n: np.ascontiguousarray(v) for n, v in a.items()}


def build(nc, ins, out):
    with ExitStack() as ctx:
        sh = Shared(nc, ctx)
        load_stage(nc, sh, ins["x"], ins["ctx"])
        attention0(nc, sh, ins["packs"], ins["ln"], ins["u"], ins["wq"], ins["lk"], ins["bq_lk"])
        mlp(nc, sh, "m0", sh.xs, ACT.Gelu, False, EPS0, ins["fc1"], ins["fc2"], ins["fc_cols"], ins["fc2_bias"])
        small_attention(nc, sh, L1, (sh.ctx_hi, sh.ctx_lo), ins["l1_w"], ins["l1_cols"], ins["l1_rows"], ins["l1_mask"],
                        None, sh.xs)
        with ExitStack() as of_layer2:
            normed = [of_layer2.enter_context(nc.sbuf_tensor(f"normed_{n}", [P, KD, C], FP32R)) for n in ("hi", "lo")]
            norm_stream_and_context(nc, sh, ins["l1_norm"], ins["ctx"], ins["l2_norm"], *normed)
            small_attention(nc, sh, L2, normed, ins["l2_w"], ins["l2_cols"], ins["l2_rows"], ins["l2_mask"],
                            ins["l2_gate"], sh.xs)
        attended = ctx.enter_context(nc.sbuf_tensor("attended", [P, XT, D], FP32))
        small_attention(nc, sh, L3, (sh.ctx_hi, sh.ctx_lo), ins["l3_w"], ins["l3_cols"], ins["l3_rows"], ins["l3_mask"],
                        None, attended)
        mlp(nc, sh, "m3", attended, ACT.Gelu_apprx_tanh, True, 1e-6, ins["mlp1"], ins["mlp2"], ins["mlp_cols"],
            ins["mlp2_bias"], out)


def kernel(**inputs):
    import concourse.bacc as _bacc
    from concourse.bass_utils import run_bass_kernel_spmd as _run

    arrays = layouts(lambda n: np.asarray(inputs[n]))
    nc = _bacc.Bacc("TRN2", target_bir_lowering=False, num_devices=1)
    ins = {n: nc.dram_tensor(f"in_{n}_dram", a.shape, mybir.dt.from_np(a.dtype), kind="ExternalInput").ap()
           for n, a in arrays.items()}
    out = nc.dram_tensor("out_0_dram", (T, D), FP32, kind="ExternalOutput").ap()
    build(nc, ins, out)
    r = _run(nc, [{f"in_{n}_dram": a for n, a in arrays.items()}], core_ids=[0])
    return r.results[0]["out_0_dram"].reshape(B, Q, D)
```
